# Optimizing a Trainium2 kernel written in Bass

```python
import numpy as np
import jax
import jax.numpy as jnp

def _softmax(x, axis=-1):
    return jax.nn.softmax(x, axis=axis)

def _gelu(x):
    return jax.nn.gelu(x, approximate=True)

def _silu(x):
    return jax.nn.silu(x)

def _sigmoid(x):
    return jax.nn.sigmoid(x)

def _layernorm(x, axis=-1, eps=1e-05):
    m = jnp.mean(x, axis=axis, keepdims=True)
    v = jnp.var(x, axis=axis, keepdims=True)
    return (x - m) / jnp.sqrt(v + eps)

def _scatter_add(tgt, idx, src, axis=0):
    return tgt.at[idx].add(src)

def _segment_sum(src, seg, n):
    return jax.ops.segment_sum(src, seg, n)
kernel_name = 'mk_adj_preln_d4_adj_r2_cd945b'

def setup_inputs(seed: int=0):
    np.random.seed(seed)
    _w = jnp.asarray

    def _rec_inputs():
        import jax
        import jax.numpy as jnp
        _gk = jax.random.key(seed)
        x = 7.22e-05 + 1 * jax.random.normal(jax.random.fold_in(_gk, 1), (64, 128, 256), jnp.float32)
        _w = (1.0 + jnp.arange(128, dtype=jnp.float32)) ** (-0.5)
        _w = _w / _w.mean()
        _pij = jnp.clip(0.0625 * _w[:, None] * _w[None, :], 0.0, 1.0)
        _a = jax.random.uniform(jax.random.fold_in(_gk, 2), (64, 128, 128)) < _pij
        _a = jnp.logical_or(_a, jnp.swapaxes(_a, -1, -2))
        _a = jnp.logical_or(_a, jnp.eye(128, dtype=bool))
        _af = _a.astype(jnp.float32)
        _af = _af * jax.random.uniform(jax.random.fold_in(_gk, 3), (64, 128, 128), jnp.float32, 0.05, 1)
        adj = _af
        return (x, adj)
    x, adj = _rec_inputs()

    def _L0_gnn_setup():
        import jax, jax.numpy as jnp
        import numpy as np
        B, N, D = (8, 1024, 256)
        key = jax.random.key(seed)
        ks = jax.random.split(key, 8)
        scale = 0.5 / np.sqrt(D)
        x = jax.random.normal(ks[0], (B, N, D), dtype=jnp.float32)
        adj = jax.random.uniform(ks[1], (B, N, N), dtype=jnp.float32)
        Wq_w = jax.random.normal(ks[2], (D, D), dtype=jnp.float32) * scale
        Wk_w = jax.random.normal(ks[3], (D, D), dtype=jnp.float32) * scale
        Wv_w = jax.random.normal(ks[4], (D, D), dtype=jnp.float32) * scale
        Wq_b = jnp.zeros((D,), dtype=jnp.float32)
        Wk_b = jnp.zeros((D,), dtype=jnp.float32)
        Wv_b = jnp.zeros((D,), dtype=jnp.float32)
        return {'x': x, 'adj': adj, 'Wq_w': Wq_w, 'Wq_b': Wq_b, 'Wk_w': Wk_w, 'Wk_b': Wk_b, 'Wv_w': Wv_w, 'Wv_b': Wv_b}
    _L0_gnn_all = _L0_gnn_setup()
    _L0_gnn_in = {k: v for k, v in _L0_gnn_all.items() if k in ('Wq_w', 'Wq_b', 'Wk_w', 'Wk_b', 'Wv_w', 'Wv_b')}
    del _L0_gnn_all

    def _L1_gnn_setup():
        import jax, jax.numpy as jnp
        import numpy as np
        B, N, DIN, DOUT, K = (4, 1024, 256, 256, 3)
        key = jax.random.key(seed)
        ks = jax.random.split(key, 8)
        X = jax.random.normal(ks[0], (B, N, DIN), dtype=jnp.float32)
        A = jax.random.uniform(ks[1], (B, N, N), dtype=jnp.float32)
        Wv = jax.random.normal(ks[2], (DIN, DOUT), dtype=jnp.float32) * 0.02
        bv = jax.random.normal(ks[3], (DOUT,), dtype=jnp.float32) * 0.02
        aw = jax.random.normal(ks[4], (2 * DOUT, 1), dtype=jnp.float32) * 0.05
        ab = jax.random.normal(ks[5], (1,), dtype=jnp.float32) * 0.05
        Wk = jax.random.normal(ks[6], (K, DIN, DOUT), dtype=jnp.float32) * 0.02
        bk = jax.random.normal(ks[7], (K, DOUT), dtype=jnp.float32) * 0.02
        return {'X': X, 'A': A, 'Wv': Wv, 'bv': bv, 'aw': aw, 'ab': ab, 'Wk': Wk, 'bk': bk}
    _L1_gnn_all = _L1_gnn_setup()
    _L1_gnn_in = {k: v for k, v in _L1_gnn_all.items() if k in ('Wv', 'bv', 'aw', 'ab', 'Wk', 'bk')}
    del _L1_gnn_all

    def _L2_gnn_setup():
        import jax, jax.numpy as jnp
        import numpy as np
        IN_F = 256
        OUT_F = 256
        ALPHA = 0.2
        NEG_INF = -9000000000000000.0
        key = jax.random.key(seed)
        k1, k2, k3, k4 = jax.random.split(key, 4)
        B, S = (8, 1024)
        hidden_state = jax.random.normal(k1, (B, S, IN_F), dtype=jnp.float32)
        adjacent_matrix = jax.random.uniform(k2, (B, S, S), dtype=jnp.float32)
        bound = 1.0 / np.sqrt(IN_F)
        W = jax.random.uniform(k3, (IN_F, OUT_F), dtype=jnp.float32, minval=-bound, maxval=bound)
        a_bound = 1.414 * np.sqrt(6.0 / (2 * OUT_F + 1))
        a = jax.random.uniform(k4, (2 * OUT_F, 1), dtype=jnp.float32, minval=-a_bound, maxval=a_bound)
        return {'hidden_state': hidden_state, 'adjacent_matrix': adjacent_matrix, 'W': W, 'a': a}
    _L2_gnn_all = _L2_gnn_setup()
    _L2_gnn_in = {k: v for k, v in _L2_gnn_all.items() if k in ('W', 'a')}
    del _L2_gnn_all

    def _L3_gnn_setup():
        import jax, jax.numpy as jnp
        import numpy as np
        IN_DIM = 256
        ATT_DIM = 64
        B, N = (4, 2048)
        key = jax.random.key(seed)
        k1, k2, k3, k4 = jax.random.split(key, 4)
        x = jax.random.normal(k1, (B, N, IN_DIM), dtype=jnp.float32)
        adj_matrix = (jax.random.uniform(k2, (B, N, N)) < 0.05).astype(jnp.float32)
        W_qk = jax.random.normal(k3, (2 * ATT_DIM, IN_DIM), dtype=jnp.float32) / np.sqrt(IN_DIM)
        W_v = jax.random.normal(k4, (IN_DIM, IN_DIM), dtype=jnp.float32) / np.sqrt(IN_DIM)
        return {'x': x, 'adj_matrix': adj_matrix, 'W_qk': W_qk, 'W_v': W_v}
    _L3_gnn_all = _L3_gnn_setup()
    _L3_gnn_in = {k: v for k, v in _L3_gnn_all.items() if k in ('W_qk', 'W_v')}
    del _L3_gnn_all
    return {'x': x, 'adj': adj, 'L0_gnn_Wq_w': _L0_gnn_in['Wq_w'], 'L0_gnn_Wq_b': _L0_gnn_in['Wq_b'], 'L0_gnn_Wk_w': _L0_gnn_in['Wk_w'], 'L0_gnn_Wk_b': _L0_gnn_in['Wk_b'], 'L0_gnn_Wv_w': _L0_gnn_in['Wv_w'], 'L0_gnn_Wv_b': _L0_gnn_in['Wv_b'], 'L1_gnn_Wv': _L1_gnn_in['Wv'], 'L1_gnn_bv': _L1_gnn_in['bv'], 'L1_gnn_aw': _L1_gnn_in['aw'], 'L1_gnn_ab': _L1_gnn_in['ab'], 'L1_gnn_Wk': _L1_gnn_in['Wk'], 'L1_gnn_bk': _L1_gnn_in['bk'], 'L2_gnn_W': _L2_gnn_in['W'], 'L2_gnn_a': _L2_gnn_in['a'], 'L3_gnn_W_qk': _L3_gnn_in['W_qk'], 'L3_gnn_W_v': _L3_gnn_in['W_v']}

def reference(x, adj, L0_gnn_Wq_w, L0_gnn_Wq_b, L0_gnn_Wk_w, L0_gnn_Wk_b, L0_gnn_Wv_w, L0_gnn_Wv_b, L1_gnn_Wv, L1_gnn_bv, L1_gnn_aw, L1_gnn_ab, L1_gnn_Wk, L1_gnn_bk, L2_gnn_W, L2_gnn_a, L3_gnn_W_qk, L3_gnn_W_v):
    import jax
    import jax.numpy as jnp

    def _L0_gnn_ref(x, adj, Wq_w, Wq_b, Wk_w, Wk_b, Wv_w, Wv_b):
        import jax, jax.numpy as jnp
        import numpy as np
        B, N, D = (8, 1024, 256)
        query = jnp.einsum('bnd,od->bno', x, Wq_w) + Wq_b
        keyt = jnp.einsum('bnd,od->bno', x, Wk_w) + Wk_b
        value = jnp.einsum('bnd,od->bno', x, Wv_w) + Wv_b
        weight = jnp.einsum('bqd,bkd->bqk', query, keyt)
        weight = adj * jnp.exp(weight)
        weight = weight / jnp.sum(weight, axis=2, keepdims=True)
        return jnp.einsum('bqk,bkd->bqd', weight, value)

    def _L1_gnn_ref(X, A, Wv, bv, aw, ab, Wk, bk):
        import jax, jax.numpy as jnp
        import numpy as np
        B, N, DIN, DOUT, K = (4, 1024, 256, 256, 3)
        d = Wv.shape[1]
        Xw = X @ Wv + bv
        sj = Xw @ aw[:d, 0]
        si = Xw @ aw[d:, 0]
        e = jax.nn.leaky_relu(sj[:, None, :] + si[:, :, None] + ab[0], negative_slope=0.2)
        alpha_matrix = A * jnp.exp(e)
        transition = alpha_matrix / (jnp.sum(alpha_matrix, axis=-1, keepdims=True) + 1e-12)
        H = jnp.zeros(X.shape[:-1] + (d,), dtype=X.dtype)
        Xk = X
        for k in range(Wk.shape[0]):
            H = H + Xk @ Wk[k] + bk[k]
            Xk = jnp.einsum('bij,bjd->bid', transition, Xk)
        return jax.nn.relu(H)

    def _L2_gnn_ref(hidden_state, adjacent_matrix, W, a):
        import jax, jax.numpy as jnp
        import numpy as np
        IN_F = 256
        OUT_F = 256
        ALPHA = 0.2
        NEG_INF = -9000000000000000.0
        Wh = jnp.einsum('bsi,io->bso', hidden_state, W)
        Wh1 = Wh @ a[:OUT_F, :]
        Wh2 = Wh @ a[OUT_F:, :]
        e = Wh1 + jnp.swapaxes(Wh2, 1, 2)
        e = jax.nn.leaky_relu(e, negative_slope=ALPHA)
        attention = jnp.where(adjacent_matrix > 0.5, e, NEG_INF)
        attention = jax.nn.softmax(attention, axis=1)
        h_prime = jnp.einsum('bst,bto->bso', attention, Wh)
        return jax.nn.elu(h_prime)

    def _L3_gnn_ref(x, adj_matrix, W_qk, W_v):
        import jax, jax.numpy as jnp
        import numpy as np
        IN_DIM = 256
        ATT_DIM = 64
        B, N = (4, 2048)
        qk = jnp.einsum('bnd,ed->bne', x, W_qk)
        q, k = jnp.split(qk, 2, axis=-1)
        v = jnp.einsum('bnd,ed->bne', x, W_v)
        inv_scale = 1.0 / ATT_DIM ** 0.5
        scores = jnp.einsum('bnd,bmd->bnm', q, k) * inv_scale
        w = jnp.sum(scores * adj_matrix, axis=-1, keepdims=True)
        w = jax.nn.softmax(w, axis=1)
        return w * v
    h = jnp.maximum(_layernorm(x, axis=-1), 0.0)
    x = x + _L0_gnn_ref(h, adj, L0_gnn_Wq_w, L0_gnn_Wq_b, L0_gnn_Wk_w, L0_gnn_Wk_b, L0_gnn_Wv_w, L0_gnn_Wv_b)
    h = jnp.maximum(_layernorm(x, axis=-1), 0.0)
    x = x + _L1_gnn_ref(h, adj, L1_gnn_Wv, L1_gnn_bv, L1_gnn_aw, L1_gnn_ab, L1_gnn_Wk, L1_gnn_bk)
    h = jnp.maximum(_layernorm(x, axis=-1), 0.0)
    x = x + _L2_gnn_ref(h, adj, L2_gnn_W, L2_gnn_a)
    h = jnp.maximum(_layernorm(x, axis=-1), 0.0)
    x = x + _L3_gnn_ref(h, adj, L3_gnn_W_qk, L3_gnn_W_v)
    return x

_drawn_inputs = setup_inputs


def setup_inputs(seed=0):
    import zlib

    import numpy as np

    out = dict(_drawn_inputs(seed))
    spreads = {'L0_gnn_Wq_b': (0.0, 0.1), 'L0_gnn_Wk_b': (0.0, 2.0), 'L0_gnn_Wv_b': (0.0, 0.1)}
    factors = {'L1_gnn_Wv': 8.0, 'L1_gnn_bv': 27.193, 'L1_gnn_aw': 8.0, 'L1_gnn_bk': 2.674}
    for name, (base, spread) in spreads.items():
        noise = np.random.default_rng([zlib.crc32(name.encode()), seed]).standard_normal(out[name].shape)
        drawn = base * np.exp(spread * noise) if base else spread * noise
        out[name] = jnp.asarray(drawn.astype(out[name].dtype))
    for name, factor in factors.items():
        out[name] = (out[name] * factor).astype(out[name].dtype)
    return out
```

```python
from contextlib import ExitStack

import concourse.bass as bass
from concourse import mybir

ALU = mybir.AluOpType
ACT = mybir.ActivationFunctionType
AX = mybir.AxisListType
F32 = mybir.dt.float32
F32R = mybir.dt.float32r

P = 128
LN_EPS = 1e-5
ROWSUM_EPS = 1e-12
SLOPE = 0.2
MASKED = -9e15
MASKED_Z = MASKED / SLOPE
G = 2
PAIRS = 32
STAGES = 4

D_ = 256
V0, HOP2, WH, HOP1, HOP0, VQK, KQ = 0, 258, 516, 774, 1030, 1286, 1670
W_COLS = 1926
S_WK, S_WQ, S_BQ, S_BK, S_WV1, S_A1, S_BV1, S_WG, S_AG = 0, 256, 512, 513, 514, 770, 772, 773, 1029
S_COLS = 1031


def pair(t, at):
    return 2 * t + at, at % 2


def exists(p):
    return not isinstance(p, int) or p >= 0


def upto(count):
    return min(count, PAIRS) if isinstance(count, int) else count


def held(eng, count):
    return count if isinstance(count, int) else eng.snap(count)


def loads(t, at):
    return 16 * (t + at // 2) + 16


def split_product(pe, out, stationary, stationary_parts, moving, moving_parts, stop=True):
    (s_hi, s_lo), (m_hi, m_lo) = stationary_parts, moving_parts
    terms = ((s_hi, m_hi), (s_hi, m_lo), (s_lo, m_hi))
    for c in range(2):
        for n, (a, b) in enumerate(terms):
            last = pe.matmul(out, stationary(a, c), moving(b, c), start=(c == 0 and n == 0),
                             stop=(stop and c == 1 and n == 2))
    return last


def graph_layers_kernel(nc: bass.Bass, x_in, adj_in, adjT_in, weights_in, setup_in, hop_bias_in, value_bias_in,
                        ab_in, y_out):
    pairs, N, _, D = x_in.shape
    assert pairs == PAIRS and N == P and D == D_
    C = D // P
    ATT = 64
    QK = 2 * ATT
    INV_SCALE = ATT ** -0.5

    with ExitStack() as ctx:
        def sb(name, *shape, dt=F32):
            return ctx.enter_context(nc.sbuf_tensor(name, [P, *shape], dt))

        def sem(name):
            return ctx.enter_context(nc.semaphore(name))

        ident = sb("ident", P)
        minus_half = sb("minus_half", G)
        ones_r = sb("ones_r", P, dt=F32R)
        w_all = sb("w_all", C, W_COLS)
        w_hi = sb("w_hi", C, W_COLS, dt=F32R)
        w_lo = sb("w_lo", C, W_COLS, dt=F32R)
        w_setup = sb("w_setup", C, S_COLS)
        hop_rows = sb("hop_rows", D)
        hop_rows_hi = sb("hop_rows_hi", D, dt=F32R)
        hop_bias = sb("hop_bias", D, dt=F32R)
        value_row = sb("value_row", D)
        value_bias = sb("value_bias", G, D)
        ab_col = sb("ab_col", 1)
        kq_bias = sb("kq_bias", C)
        qk_const = sb("qk_const", 1)
        sij_const = sb("sij_const", G, 2)

        def parts(start, width):
            return w_hi[:, :, start:start + width], w_lo[:, :, start:start + width]

        w_v0, w_hop2, w_wh = parts(V0, D + 2), parts(HOP2, D + 2), parts(WH, D + 2)
        w_hop1, w_hop0, w_vqk, w_kq = parts(HOP1, D), parts(HOP0, D), parts(VQK, D + QK), parts(KQ, D)

        x0, x1, x2, x3, y, xb = (sb(n, 2, G, D) for n in ("x0", "x1", "x2", "x3", "y", "xb"))
        adjT0, adj1, adjT2 = (sb(n, 2, G, N) for n in ("adjT0", "adj1", "adjT2"))
        stats0, stats1, stats2, stats3 = (sb(f"stats{n}", 2, G, 6) for n in range(4))
        moments0, moments1, moments2, moments3 = (sb(f"moments{n}", 2, G, 2) for n in range(4))
        negmean0, negmean1, negmean2, negmean3 = (sb(f"negmean{n}", 2, G) for n in range(4))
        vareps0, vareps1, vareps2, vareps3 = (sb(f"vareps{n}", 2, G) for n in range(4))
        rstd0, rstd1, rstd2, rstd3 = (sb(f"rstd{n}", 2, G) for n in range(4))
        normed0, normed1, normed2, normed3 = (sb(f"normed{n}", 2, G, D) for n in range(4))
        h0 = sb("h0", 2, C, G * N)
        h_hi0, h_hi1, h_hi2, h_hi3 = (sb(f"h_hi{n}", 2, C, G * N, dt=F32R) for n in range(4))
        h_lo0, h_lo1, h_lo2, h_lo3 = (sb(f"h_lo{n}", 2, C, G * N, dt=F32R) for n in range(4))
        keyq_sb = sb("keyq_sb", 2, C, G * N)
        val0_sb = sb("val0_sb", 2, G, D + 2)
        kbias, rowinv0 = sb("kbias", 2, G), sb("rowinv0", 2, G)
        exp0, att0 = sb("exp0", 2, G, N), sb("att0", 2, G, N)
        hop2_sb, hop1_sb = sb("hop2_sb", 2, G, D + 2), sb("hop1_sb", 2, G, D)
        sij = sb("sij", 2, G, 2)
        z1, leaky1, exp1, alpha, trans = (sb(n, 2, G, N) for n in ("z1", "leaky1", "exp1", "alpha", "trans"))
        rowsum1, rowsum1e, rowinv1 = (sb(n, 2, G) for n in ("rowsum1", "rowsum1e", "rowinv1"))
        transT_sb = sb("transT_sb", 2, G * N)
        wh_sb = sb("wh_sb", 2, G, D + 2)
        penalty, z2, leaky2, exp2, att2 = (sb(n, 2, G, N) for n in ("penalty", "z2", "leaky2", "exp2", "att2"))
        max2, negmax2, sum2, suminv2 = (sb(n, 2, G) for n in ("max2", "negmax2", "sum2", "suminv2"))
        elu_exp, elu_pos = sb("elu_exp", 2, G, D), sb("elu_pos", 2, G, D)
        vqk_sb = sb("vqk_sb", 2, G, D + QK)
        w3_prod, w3, w3col_sb = sb("w3_prod", 2, G, ATT), sb("w3", 2, G), sb("w3col_sb", 2, G)

        def rows(name, width):
            return ctx.enter_context(nc.sbuf_tensor(name, [G, 2, width], F32))

        max3, negmax3, sum3, suminv3 = (rows(n, 1) for n in ("max3", "negmax3", "sum3", "suminv3"))
        exp3, soft3 = rows("exp3", N), rows("soft3", N)

        psum = ctx.enter_context(nc.psum_tensor("psum", [P, 8, 512], F32))
        turn0 = psum[:, 3].rearrange("p (c n) -> p c n", c=C)
        keyq = psum[:, 7].rearrange("p (c n) -> p c n", c=C)
        val0 = psum[:, 0:2]
        score0 = psum[:, 3, 0:G * N]
        mix0 = psum[:, 6:8]
        turn1 = psum[:, 4].rearrange("p (c n) -> p c n", c=C)
        hop2 = psum[:, 2:4]
        sjrow = psum[:, 2, 0:G * N]
        transT = psum[:, 0, 0:G * N]
        hop1 = psum[:, 1].rearrange("p (j d) -> p j d", j=G)
        hop0 = psum[:, 5].rearrange("p (j d) -> p j d", j=G)
        turn2 = psum[:, 7].rearrange("p (c n) -> p c n", c=C)
        wh = psum[:, 2:4]
        wh1row = psum[:, 1, 0:G * N]
        mix2 = psum[:, 1].rearrange("p (j d) -> p j d", j=G)
        turn3 = psum[:, 6].rearrange("p (c n) -> p c n", c=C)
        vqk = psum[:, 4:6]
        adjk = psum[:, 0, 0:G * ATT].rearrange("p (j d) -> p j d", j=G)
        w3row = psum[0:G, 2, 0:N]
        w3col = psum[:, 6, 0:G]

        s_setup_x = sem("setup_x")
        s_setup_w = sem("setup_w")
        s_setup_p = sem("setup_p")
        s_setup_v = sem("setup_v")
        s_load_x = [sem(f"load_x_{i}") for i in range(2)]
        s_load_adjT0 = [sem(f"load_adjT0_{i}") for i in range(2)]
        s_stat0 = sem("stat0")
        s_aggr0 = sem("aggr0")
        s_mom0 = sem("mom0")
        s_rstd0 = sem("rstd0")
        s_norm0 = sem("norm0")
        s_turn0 = sem("turn0")
        s_h0 = sem("h0")
        s_hi0 = sem("hi0")
        s_lo0 = sem("lo0")
        s_xb = sem("xb")
        s_keyq = sem("keyq")
        s_keyq_out = sem("keyq_out")
        s_val0 = sem("val0")
        s_val0_out = sem("val0_out")
        s_kbias = sem("kbias")
        s_score0 = sem("score0")
        s_exp0 = sem("exp0")
        s_att0 = sem("att0")
        s_mix0 = sem("mix0")
        s_rowinv0 = sem("rowinv0")
        s_x1 = sem("x1")
        s_load_adj1 = [sem(f"load_adj1_{i}") for i in range(2)]
        s_stat1 = sem("stat1")
        s_aggr1 = sem("aggr1")
        s_mom1 = sem("mom1")
        s_rstd1 = sem("rstd1")
        s_norm1 = sem("norm1")
        s_turn1 = sem("turn1")
        s_hi1 = sem("hi1")
        s_lo1 = sem("lo1")
        s_hop2 = sem("hop2")
        s_hop2_out = sem("hop2_out")
        s_sij = sem("sij")
        s_sjrow = sem("sjrow")
        s_z1 = sem("z1")
        s_leaky1 = sem("leaky1")
        s_exp1 = sem("exp1")
        s_alpha = sem("alpha")
        s_rowsum1e = sem("rowsum1e")
        s_rowinv1 = sem("rowinv1")
        s_trans = sem("trans")
        s_transT = sem("transT")
        s_transT_out = sem("transT_out")
        s_hop1_0 = sem("hop1_0")
        s_hop1_out = sem("hop1_out")
        s_hop0_0 = sem("hop0_0")
        s_x2 = sem("x2")
        s_load_adjT2 = [sem(f"load_adjT2_{i}") for i in range(2)]
        s_stat2 = sem("stat2")
        s_aggr2 = sem("aggr2")
        s_mom2 = sem("mom2")
        s_rstd2 = sem("rstd2")
        s_norm2 = sem("norm2")
        s_turn2 = sem("turn2")
        s_hi2 = sem("hi2")
        s_lo2 = sem("lo2")
        s_wh = sem("wh")
        s_wh_out = sem("wh_out")
        s_wh1row = sem("wh1row")
        s_z2 = sem("z2")
        s_leaky2 = sem("leaky2")
        s_max2 = sem("max2")
        s_negmax2 = sem("negmax2")
        s_exp2 = sem("exp2")
        s_suminv2 = sem("suminv2")
        s_att2 = sem("att2")
        s_mix2 = sem("mix2")
        s_elu_exp = sem("elu_exp")
        s_elu_pos = sem("elu_pos")
        s_x3 = sem("x3")
        s_stat3 = sem("stat3")
        s_aggr3 = sem("aggr3")
        s_mom3 = sem("mom3")
        s_rstd3 = sem("rstd3")
        s_norm3 = sem("norm3")
        s_turn3 = sem("turn3")
        s_hi3 = sem("hi3")
        s_lo3 = sem("lo3")
        s_vqk_0 = sem("vqk_0")
        s_vqk_out = sem("vqk_out")
        s_adjk = sem("adjk")
        s_w3 = sem("w3")
        s_w3row = sem("w3row")
        s_max3 = sem("max3")
        s_negmax3 = sem("negmax3")
        s_exp3 = sem("exp3")
        s_suminv3 = sem("suminv3")
        s_soft3 = sem("soft3")
        s_w3col = sem("w3col")
        s_w3col_out = sem("w3col_out")
        s_out = sem("out")
        s_store = [sem(f"store_{i}") for i in range(2)]

        SETUP_DMAS = 6
        SETUP_STEPS = 21
        block = ctx.enter_context(nc.Block())

        def run(eng, step):
            full_from = (STAGES + 3) // 2
            for k in range(2 * full_from):
                step(0, k, lambda g: 0 <= k - g < PAIRS)
            with eng.Fori(full_from, PAIRS // 2) as t:
                for c in range(2):
                    step(t, c, lambda g: True)
            for k in range(PAIRS, PAIRS + STAGES):
                step(0, k, lambda g: 0 <= k - g < PAIRS)

        @block.sync
        def _(sync):
            sync.dma_start(w_setup[:, :, :], setup_in).then_inc(s_setup_x, 16)
            sync.dma_start(w_all[:, :, :], weights_in).then_inc(s_setup_x, 16)
            sync.dma_start(value_row[:, :], value_bias_in.partition_broadcast(P)).then_inc(s_setup_x, 16)
            sync.dma_start(ab_col[:, :], ab_in.partition_broadcast(P)).then_inc(s_setup_x, 16)
            sync.wait_ge(s_setup_w, 1)
            for q in (0, 32):
                sync.dma_start(hop_rows[q:q + 3, :], hop_bias_in).then_inc(s_setup_x, 16)

            def step(t, at, live):
                if live(1):
                    p, s = pair(t, at - 1)
                    if exists(p - 2):
                        sync.wait_ge(s_alpha, p - 1)
                    last = sync.dma_start(adj1[:, s], adj_in[p])
                    last.then_inc(s_load_adj1[s], 16)
                if live(0):
                    p, s = pair(t, at - 0)
                    if exists(p - 2):
                        sync.wait_ge(s_xb, p - 1)
                    last = sync.dma_start(x0[:, s], x_in[p])
                    last.then_inc(s_load_x[s], 16)
                if live(0):
                    p, s = pair(t, at - 0)
                    if exists(p - 2):
                        sync.wait_ge(s_att0, p - 1)
                    last = sync.dma_start(adjT0[:, s], adjT_in[p])
                    last.then_inc(s_load_adjT0[s], 16)
                if live(2):
                    p, s = pair(t, at - 2)
                    if exists(p - 2):
                        sync.wait_ge(s_adjk, p - 1)
                    last = sync.dma_start(adjT2[:, s], adjT_in[p])
                    last.then_inc(s_load_adjT2[s], 16)
                if live(4):
                    p, s = pair(t, at - 4)
                    sync.wait_ge(s_out, p + 1)
                    last = sync.dma_start(y_out[p], y[:, s])
                    last.then_inc(s_store[s], 16)

            run(sync, step)
            for i in range(2):
                sync.wait_ge(s_store[i], 16 * (PAIRS // 2))

        @block.gpsimd
        def _(pool):
            pool.memset(hop_rows[:, :], 0.0).then_inc(s_setup_w, 1)
            pool.memset(ident[:, :], 0.0).then_inc(s_setup_w, 1)
            pool.wait_ge(s_setup_w, 2)
            pool.affine_select(out=ident[:, :], in_=ident[:, :], compare_op=ALU.not_equal, fill=1.0, base=0,
                               pattern=[[-1, P]], channel_multiplier=1).then_inc(s_setup_w, 1)
            pool.memset(minus_half[:, :], -0.5).then_inc(s_setup_w, 1)
            pool.wait_ge(s_setup_w, 4)
            pool.wait_ge(s_setup_v, SETUP_STEPS)

            def step(t, at, live):
                if live(1):
                    p, s = pair(t, at - 1)
                    last = pool.tensor_tensor(xb[:, s], x0[:, s], value_bias[:, :, :], ALU.add)
                    last.then_inc(s_xb, 1)
                if live(3):
                    p, s = pair(t, at - 3)
                    pool.wait_ge(s_mom2, p + 1)
                    last = pool.tensor_tensor(rstd2[:, s], vareps2[:, s], minus_half[:, :], ALU.pow)
                    last.then_inc(s_rstd2, 1)
                if live(3):
                    p, s = pair(t, at - 3)
                    count = held(pool, p + 1)
                    pool.wait_ge(s_setup_w, 4)
                    pool.wait_ge(s_rstd2, count)
                    for j in range(G):
                        last = pool.tensor_scalar(normed2[:, s, j], x2[:, s, j], negmean2[:, s, j:j + 1],
                                                  rstd2[:, s, j:j + 1], ALU.add, ALU.mult)
                    last.then_inc(s_norm2, 1)
                if live(4):
                    p, s = pair(t, at - 4)
                    pool.wait_ge(s_mom3, p + 1)
                    last = pool.tensor_tensor(rstd3[:, s], vareps3[:, s], minus_half[:, :], ALU.pow)
                    last.then_inc(s_rstd3, 1)
                if live(4):
                    p, s = pair(t, at - 4)
                    count = held(pool, p + 1)
                    pool.wait_ge(s_setup_w, 4)
                    pool.wait_ge(s_rstd3, count)
                    for j in range(G):
                        last = pool.tensor_scalar(normed3[:, s, j], x3[:, s, j], negmean3[:, s, j:j + 1],
                                                  rstd3[:, s, j:j + 1], ALU.add, ALU.mult)
                    last.then_inc(s_norm3, 1)
                if live(0):
                    p, s = pair(t, at - 0)
                    pool.wait_ge(s_mom0, p + 1)
                    last = pool.tensor_tensor(rstd0[:, s], vareps0[:, s], minus_half[:, :], ALU.pow)
                    last.then_inc(s_rstd0, 1)
                if live(0):
                    p, s = pair(t, at - 0)
                    count = held(pool, p + 1)
                    pool.wait_ge(s_setup_w, 4)
                    pool.wait_ge(s_rstd0, count)
                    for j in range(G):
                        last = pool.tensor_scalar(normed0[:, s, j], x0[:, s, j], negmean0[:, s, j:j + 1],
                                                  rstd0[:, s, j:j + 1], ALU.add, ALU.mult)
                    last.then_inc(s_norm0, 1)
                if live(1):
                    p, s = pair(t, at - 1)
                    pool.wait_ge(s_mom1, p + 1)
                    last = pool.tensor_tensor(rstd1[:, s], vareps1[:, s], minus_half[:, :], ALU.pow)
                    last.then_inc(s_rstd1, 1)
                if live(1):
                    p, s = pair(t, at - 1)
                    count = held(pool, p + 1)
                    pool.wait_ge(s_setup_w, 4)
                    pool.wait_ge(s_rstd1, count)
                    for j in range(G):
                        last = pool.tensor_scalar(normed1[:, s, j], x1[:, s, j], negmean1[:, s, j:j + 1],
                                                  rstd1[:, s, j:j + 1], ALU.add, ALU.mult)
                    last.then_inc(s_norm1, 1)
                if live(0):
                    p, s = pair(t, at - 0)
                    pool.wait_ge(s_hi0, p + 1)
                    last = pool.tensor_tensor(h_lo0[:, s], h0[:, s], h_hi0[:, s].bitcast(F32), ALU.subtract)
                    last.then_inc(s_lo0, 1)

            run(pool, step)

        @block.scalar
        def _(act):
            act.wait_ge(s_setup_v, SETUP_STEPS)

            def step(t, at, live):
                if live(4):
                    p, s = pair(t, at - 4)
                    act.wait_ge(s_turn3, p + 1)
                    last = act.activation(h_hi3[:, s], turn3, ACT.Relu)
                    last.then_inc(s_hi3, 1)
                if live(2):
                    p, s = pair(t, at - 2)
                    act.wait_ge(s_leaky1, p + 1)
                    last = act.activation(exp1[:, s], leaky1[:, s], ACT.Exp)
                    last.then_inc(s_exp1, 1)
                if live(3):
                    p, s = pair(t, at - 3)
                    act.wait_ge(s_wh, p + 1)
                    last = act.activation(wh_sb[:, s], wh[:, :, 0:D + 2], ACT.Copy)
                    last.then_inc(s_wh_out, 1)
                if live(2):
                    p, s = pair(t, at - 2)
                    act.wait_ge(s_transT, p + 1)
                    last = act.activation(transT_sb[:, s], transT, ACT.Copy)
                    last.then_inc(s_transT_out, 1)
                if live(4):
                    p, s = pair(t, at - 4)
                    act.wait_ge(s_vqk_0, p + 1)
                    last = act.activation(vqk_sb[:, s], vqk[:, :, 0:D + QK], ACT.Copy)
                    last.then_inc(s_vqk_out, 1)
                if live(3):
                    p, s = pair(t, at - 3)
                    act.wait_ge(s_negmax2, p + 1)
                    for j in range(G):
                        last = act.activation(exp2[:, s, j], leaky2[:, s, j], ACT.Exp, bias=negmax2[:, s, j:j + 1],
                                              accum_out=sum2[:, s, j:j + 1])
                    last.then_inc(s_exp2, 1)
                if live(2):
                    p, s = pair(t, at - 2)
                    act.wait_ge(s_hop1_0, p + 1)
                    last = act.activation(hop1_sb[:, s], hop1, ACT.Copy)
                    last.then_inc(s_hop1_out, 1)
                if live(0):
                    p, s = pair(t, at - 0)
                    act.wait_ge(s_turn0, p + 1)
                    last = act.activation(h0[:, s], turn0, ACT.Relu)
                    last.then_inc(s_h0, 1)
                if live(3):
                    p, s = pair(t, at - 3)
                    act.wait_ge(s_mix2, p + 1)
                    last = act.activation(elu_exp[:, s], mix2, ACT.Exp)
                    last.then_inc(s_elu_exp, 1)
                if live(1):
                    p, s = pair(t, at - 1)
                    act.wait_ge(s_turn1, p + 1)
                    last = act.activation(h_hi1[:, s], turn1, ACT.Relu)
                    last.then_inc(s_hi1, 1)
                if live(4):
                    p, s = pair(t, at - 4)
                    act.wait_ge(s_negmax3, p + 1)
                    last = act.activation(exp3[:, s], w3row, ACT.Exp, bias=negmax3[:, s], accum_out=sum3[:, s])
                    last.then_inc(s_exp3, 1)
                if live(1):
                    p, s = pair(t, at - 1)
                    act.wait_ge(s_hop2, p + 1)
                    last = act.activation(hop2_sb[:, s], hop2[:, :, 0:D + 2], ACT.Copy)
                    last.then_inc(s_hop2_out, 1)
                if live(0):
                    p, s = pair(t, at - 0)
                    act.wait_ge(s_keyq, p + 1)
                    for m in range(C):
                        last = act.activation(keyq_sb[:, s, m, :], keyq[:, m, :], ACT.Identity, bias=kq_bias[:, m:m + 1])
                    last.then_inc(s_keyq_out, 1)
                if live(0):
                    p, s = pair(t, at - 0)
                    act.wait_ge(s_val0, p + 1)
                    last = act.activation(val0_sb[:, s, :, 0:D + 1], val0[:, :, 0:D + 1], ACT.Copy)
                    last.then_inc(s_val0_out, 1)
                if live(4):
                    p, s = pair(t, at - 4)
                    act.wait_ge(s_w3col, p + 1)
                    last = act.activation(w3col_sb[:, s], w3col, ACT.Copy)
                    last.then_inc(s_w3col_out, 1)
                if live(2):
                    p, s = pair(t, at - 2)
                    act.wait_ge(s_turn2, p + 1)
                    last = act.activation(h_hi2[:, s], turn2, ACT.Relu)
                    last.then_inc(s_hi2, 1)
                if live(1):
                    p, s = pair(t, at - 1)
                    act.wait_ge(s_sij, p + 1)
                    act.wait_ge(s_sjrow, p + 1)
                    for j in range(G):
                        last = act.activation(z1[:, s, j], sjrow[:, N * j:N * (j + 1)], ACT.Identity, bias=sij[:, s, j, 0:1])
                    last.then_inc(s_z1, 1)
                if live(0):
                    p, s = pair(t, at - 0)
                    act.wait_ge(s_kbias, p + 1)
                    act.wait_ge(s_score0, p + 1)
                    for j in range(G):
                        last = act.activation(exp0[:, s, j], score0[:, N * j:N * (j + 1)], ACT.Exp, bias=kbias[:, s, j:j + 1])
                    last.then_inc(s_exp0, 1)

            run(act, step)

        @block.tensor
        def _(pe):
            pe.wait_ge(s_setup_x, 16 * SETUP_DMAS)
            for m in range(C):
                for c in range(C):
                    pe.matmul(psum[:, m, 0:D + 1], w_setup[:, c, S_WK + P * m:S_WK + P * (m + 1)],
                              w_setup[:, c, S_WQ:S_WQ + D + 1], start=(c == 0), stop=(c == C - 1))
            small = psum[:, 2]
            for m in range(C):
                for c in range(C):
                    pe.matmul(small[:, m:m + 1], w_setup[:, c, S_WQ + P * m:S_WQ + P * (m + 1)],
                              w_setup[:, c, S_BK:S_BK + 1], start=(c == 0), stop=(c == C - 1))
            for c in range(C):
                pe.matmul(small[:, 2:3], w_setup[:, c, S_BK:S_BK + 1].broadcast_to([P, P]),
                          w_setup[:, c, S_BQ:S_BQ + 1], start=(c == 0), stop=(c == C - 1))
            for c in range(C):
                pe.matmul(small[:, 4:6], w_setup[:, c, S_BV1:S_BV1 + 1].broadcast_to([P, P]),
                          w_setup[:, c, S_A1:S_A1 + 2], start=(c == 0), stop=(c == C - 1))
            for m in range(C):
                for start, vectors, to in ((S_WV1, S_A1, 8), (S_WG, S_AG, 12)):
                    for c in range(C):
                        last = pe.matmul(small[:, to + 2 * m:to + 2 * m + 2],
                                         w_setup[:, c, start + P * m:start + P * (m + 1)],
                                         w_setup[:, c, vectors:vectors + 2], start=(c == 0), stop=(c == C - 1))
            last.then_inc(s_setup_p, 1)
            pe.wait_ge(s_setup_w, 3)
            pe.wait_ge(s_setup_v, SETUP_STEPS)

            def step(t, at, live):
                if live(3):
                    p, s = pair(t, at - 3)
                    pe.wait_ge(s_keyq_out, upto(p + 3))
                    pe.wait_ge(s_norm2, p + 1)
                    for j in range(G):
                        for c in range(C):
                            last = pe.transpose(turn2[:, c, N * j:N * (j + 1)], normed2[:, s, j, P * c:P * (c + 1)],
                                                ident[:, :])
                    last.then_inc(s_turn2, 1)
                if live(2):
                    p, s = pair(t, at - 2)
                    pe.wait_ge(s_sij, p + 1)
                    for j in range(G):
                        last = pe.transpose(sjrow[:, N * j:N * (j + 1)], sij[:, s, j, 1:2].broadcast_to([N, P]), ident[:, :])
                    last.then_inc(s_sjrow, 1)
                if live(1):
                    p, s = pair(t, at - 1)
                    pe.wait_ge(s_keyq_out, p + 1)
                    for j in range(G):
                        for c in range(C):
                            last = pe.matmul(score0[:, N * j:N * (j + 1)], keyq_sb[:, s, c, N * j:N * (j + 1)],
                                             h0[:, s, c, N * j:N * (j + 1)], start=(c == 0), stop=(c == C - 1))
                    last.then_inc(s_score0, 1)
                if live(4):
                    p, s = pair(t, at - 4)
                    pe.wait_ge(s_norm3, p + 1)
                    if exists(p - 1):
                        pe.wait_ge(s_w3col_out, p)
                    for j in range(G):
                        for c in range(C):
                            last = pe.transpose(turn3[:, c, N * j:N * (j + 1)], normed3[:, s, j, P * c:P * (c + 1)],
                                                ident[:, :])
                    last.then_inc(s_turn3, 1)
                if live(3):
                    p, s = pair(t, at - 3)
                    pe.wait_ge(s_exp0, upto(p + 3))
                    pe.wait_ge(s_z1, upto(p + 2))
                    pe.wait_ge(s_lo2, p + 1)
                    for j in range(G):
                        last = split_product(pe, wh[:, j, 0:D + 2], lambda h, c: h[:, s, c, N * j:N * (j + 1)], (h_hi2, h_lo2),
                                             lambda w, c: w[:, c, :], w_wh)
                    last.then_inc(s_wh, 1)
                if live(1):
                    p, s = pair(t, at - 1)
                    pe.wait_ge(s_att0, p + 1)
                    if exists(p - 3):
                        pe.wait_ge(s_lo3, p - 2)
                    for j in range(G):
                        last = pe.matmul(mix0[:, j, 0:D + 2], att0[:, s, j], val0_sb[:, s, j, :], start=True, stop=True)
                    last.then_inc(s_mix0, 1)
                if live(4):
                    p, s = pair(t, at - 4)
                    pe.wait_ge(s_lo3, p + 1)
                    last = split_product(pe, vqk[:, 1, 0:D + QK], lambda h, c: h[:, s, c, N * 1:N * 2], (h_hi3, h_lo3),
                                         lambda w, c: w[:, c, :], w_vqk)
                if live(3):
                    p, s = pair(t, at - 3)
                    pe.wait_ge(s_wh_out, p + 1)
                    for j in range(G):
                        last = pe.transpose(wh1row[:, N * j:N * (j + 1)], wh_sb[:, s, j, D:D + 1].broadcast_to([N, P]), ident[:, :])
                    last.then_inc(s_wh1row, 1)
                if live(2):
                    p, s = pair(t, at - 2)
                    pe.wait_ge(s_trans, p + 1)
                    for j in range(G):
                        last = pe.transpose(transT[:, N * j:N * (j + 1)], trans[:, s, j], ident[:, :])
                    last.then_inc(s_transT, 1)
                if live(4):
                    p, s = pair(t, at - 4)
                    last = split_product(pe, vqk[:, 0, 0:D + QK], lambda h, c: h[:, s, c, N * 0:N * 1], (h_hi3, h_lo3),
                                         lambda w, c: w[:, c, :], w_vqk)
                    last.then_inc(s_vqk_0, 1)
                if live(2):
                    p, s = pair(t, at - 2)
                    pe.wait_ge(s_transT_out, p + 1)
                    if exists(p - 1):
                        pe.wait_ge(s_z2, p)
                    split_product(pe, hop1[:, 1, :], lambda h, c: h[:, s, c, N * 1:N * 2], (h_hi1, h_lo1),
                                  lambda w, c: w[:, c, :], w_hop1, stop=False)
                    last = pe.matmul(hop1[:, 1, :], transT_sb[:, s, N * 1:N * 2], hop2_sb[:, s, 1, 0:D], start=False, stop=True)
                if live(4):
                    p, s = pair(t, at - 4)
                    pe.wait_ge(s_vqk_out, p + 1)
                    for j in range(G):
                        last = pe.matmul(adjk[:, j, :], adjT2[:, s, j], vqk_sb[:, s, j, D + ATT:D + 2 * ATT], start=True, stop=True)
                    last.then_inc(s_adjk, 1)
                if live(2):
                    p, s = pair(t, at - 2)
                    split_product(pe, hop1[:, 0, :], lambda h, c: h[:, s, c, N * 0:N * 1], (h_hi1, h_lo1),
                                  lambda w, c: w[:, c, :], w_hop1, stop=False)
                    last = pe.matmul(hop1[:, 0, :], transT_sb[:, s, N * 0:N * 1], hop2_sb[:, s, 0, 0:D], start=False, stop=True)
                    last.then_inc(s_hop1_0, 1)
                if live(0):
                    p, s = pair(t, at - 0)
                    pe.wait_ge(s_norm0, p + 1)
                    for j in range(G):
                        for c in range(C):
                            last = pe.transpose(turn0[:, c, N * j:N * (j + 1)], normed0[:, s, j, P * c:P * (c + 1)],
                                                ident[:, :])
                    last.then_inc(s_turn0, 1)
                if live(3):
                    p, s = pair(t, at - 3)
                    pe.wait_ge(s_hop1_out, upto(p + 2))
                    pe.wait_ge(s_att2, p + 1)
                    for j in range(G):
                        last = pe.matmul(mix2[:, j, :], att2[:, s, j], wh_sb[:, s, j, 0:D], start=True, stop=True)
                    last.then_inc(s_mix2, 1)
                if live(4):
                    p, s = pair(t, at - 4)
                    pe.wait_ge(s_w3, p + 1)
                    last = pe.transpose(w3row, w3[:, s], ident[:, :])
                    last.then_inc(s_w3row, 1)
                if live(2):
                    p, s = pair(t, at - 2)
                    pe.wait_ge(s_hop1_out, p + 1)
                    split_product(pe, hop0[:, 1, :], lambda h, c: h[:, s, c, N * 1:N * 2], (h_hi1, h_lo1),
                                  lambda w, c: w[:, c, :], w_hop0, stop=False)
                    pe.matmul(hop0[:, 1, :], ones_r[:, :], hop_bias[:, :], start=False, stop=False)
                    last = pe.matmul(hop0[:, 1, :], transT_sb[:, s, N * 1:N * 2], hop1_sb[:, s, 1], start=False, stop=True)
                if live(1):
                    p, s = pair(t, at - 1)
                    pe.wait_ge(s_norm1, p + 1)
                    for j in range(G):
                        for c in range(C):
                            last = pe.transpose(turn1[:, c, N * j:N * (j + 1)], normed1[:, s, j, P * c:P * (c + 1)],
                                                ident[:, :])
                    last.then_inc(s_turn1, 1)
                if live(2):
                    p, s = pair(t, at - 2)
                    split_product(pe, hop0[:, 0, :], lambda h, c: h[:, s, c, N * 0:N * 1], (h_hi1, h_lo1),
                                  lambda w, c: w[:, c, :], w_hop0, stop=False)
                    pe.matmul(hop0[:, 0, :], ones_r[:, :], hop_bias[:, :], start=False, stop=False)
                    last = pe.matmul(hop0[:, 0, :], transT_sb[:, s, N * 0:N * 1], hop1_sb[:, s, 0], start=False, stop=True)
                    last.then_inc(s_hop0_0, 1)
                if live(0):
                    p, s = pair(t, at - 0)
                    pe.wait_ge(s_hi0, p + 1)
                    pe.wait_ge(s_lo0, p + 1)
                    for m in range(C):
                        last = split_product(pe, keyq[:, m, :], lambda w, c: w[:, c, P * m:P * (m + 1)], w_kq,
                                             lambda h, c: h[:, s, c, :], (h_hi0, h_lo0))
                    last.then_inc(s_keyq, 1)
                if live(1):
                    p, s = pair(t, at - 1)
                    pe.wait_ge(s_lo1, p + 1)
                    if exists(p - 3):
                        pe.wait_ge(s_exp3, p - 2)
                    for j in range(G):
                        last = split_product(pe, hop2[:, j, 0:D + 2], lambda h, c: h[:, s, c, N * j:N * (j + 1)], (h_hi1, h_lo1),
                                             lambda w, c: w[:, c, :], w_hop2)
                    last.then_inc(s_hop2, 1)
                if live(0):
                    p, s = pair(t, at - 0)
                    for j in range(G):
                        last = split_product(pe, val0[:, j, 0:D + 2], lambda h, c: h[:, s, c, N * j:N * (j + 1)], (h_hi0, h_lo0),
                                             lambda w, c: w[:, c, :], w_v0)
                    last.then_inc(s_val0, 1)
                if live(4):
                    p, s = pair(t, at - 4)
                    count = held(pe, p + 1)
                    pe.wait_ge(s_setup_w, 3)
                    pe.wait_ge(s_soft3, count)
                    last = pe.transpose(w3col, soft3[:, s], ident[0:G, 0:G])
                    last.then_inc(s_w3col, 1)

            run(pe, step)

        @block.vector
        def _(vec):
            steps = [0]

            def setup(instruction, wait=False):
                steps[0] += 1
                instruction.then_inc(s_setup_v, 1)
                if wait:
                    vec.wait_ge(s_setup_v, steps[0])

            setup(vec.memset(ones_r[:, :].bitcast(F32), 1.0))
            setup(vec.memset(hop_bias[64:P, :].bitcast(F32), 0.0))
            for s in range(2):
                setup(vec.memset(val0_sb[:, s, :, D + 1], 1.0))
            vec.wait_ge(s_setup_x, 16 * SETUP_DMAS)
            for j in range(G):
                setup(vec.tensor_scalar(value_bias[:, j, :], value_row[:, :], -1.0, None, ALU.add))
            setup(vec.tensor_copy(hop_bias[0:32, :], hop_rows[0:32, :]))
            setup(vec.tensor_copy(hop_rows_hi[32:64, :], hop_rows[32:64, :]), wait=True)
            setup(vec.tensor_tensor(hop_bias[32:64, :], hop_rows[32:64, :], hop_rows_hi[32:64, :].bitcast(F32),
                                    ALU.subtract))
            vec.wait_ge(s_setup_p, 1)
            small = psum[:, 2]
            setup(vec.tensor_copy(kq_bias[:, :], small[:, 0:C]))
            setup(vec.tensor_copy(qk_const[:, :], small[:, 2:3]))
            for j in range(G):
                setup(vec.tensor_scalar(sij_const[:, j, 0:1], small[:, 4:5], ab_col[:, 0:1], None, ALU.add))
                setup(vec.tensor_copy(sij_const[:, j, 1:2], small[:, 5:6]))
            setup(vec.tensor_copy(w_all[:, :, KQ:KQ + D], psum[:, 0:C, 0:D]))
            setup(vec.tensor_copy(w_all[:, :, V0 + D], psum[:, 0:C, D]))
            for start, to in ((8, HOP2 + D), (12, WH + D)):
                setup(vec.tensor_copy(w_all[:, :, to:to + 2],
                                      small[:, start:start + 2 * C].rearrange("p (m v) -> p m v", m=C)), wait=True)
            setup(vec.tensor_copy(w_hi[:, :, :], w_all[:, :, :]), wait=True)
            setup(vec.tensor_tensor(w_lo[:, :, :], w_all[:, :, :], w_hi[:, :, :].bitcast(F32), ALU.subtract), wait=True)
            assert steps[0] == SETUP_STEPS, steps

            def step(t, at, live):
                if live(2):
                    p, s = pair(t, at - 2)
                    vec.wait_ge(s_z1, p + 1)
                    last = vec.scalar_tensor_tensor(leaky1[:, s], z1[:, s], SLOPE, z1[:, s], ALU.mult, ALU.max)
                    last.then_inc(s_leaky1, 1)
                if live(1):
                    p, s = pair(t, at - 1)
                    vec.wait_ge(s_exp0, p + 1)
                    vec.wait_ge(s_load_adjT0[s], loads(t, at - 1))
                    last = vec.tensor_tensor(att0[:, s], exp0[:, s], adjT0[:, s], ALU.mult)
                    last.then_inc(s_att0, 1)
                if live(4):
                    p, s = pair(t, at - 4)
                    vec.wait_ge(s_hi3, p + 1)
                    vec.wait_ge(s_turn3, p + 1)
                    last = vec.scalar_tensor_tensor(h_lo3[:, s], turn3, 0.0, h_hi3[:, s].bitcast(F32), ALU.max, ALU.subtract)
                    last.then_inc(s_lo3, 1)
                if live(2):
                    p, s = pair(t, at - 2)
                    vec.wait_ge(s_exp1, p + 1)
                    vec.wait_ge(s_load_adj1[s], loads(t, at - 2))
                    for j in range(G):
                        last = vec.scalar_tensor_tensor(alpha[:, s, j], exp1[:, s, j], 1.0, adj1[:, s, j], ALU.mult, ALU.mult,
                                                        accum_out=rowsum1[:, s, j:j + 1])
                    last.then_inc(s_alpha, 1)
                if live(2):
                    p, s = pair(t, at - 2)
                    vec.wait_ge(s_alpha, p + 1)
                    last = vec.tensor_scalar(rowsum1e[:, s], rowsum1[:, s], ROWSUM_EPS, None, ALU.add)
                    last.then_inc(s_rowsum1e, 1)
                if live(2):
                    p, s = pair(t, at - 2)
                    vec.wait_ge(s_rowsum1e, p + 1)
                    last = vec.reciprocal(rowinv1[:, s], rowsum1e[:, s])
                    last.then_inc(s_rowinv1, 1)
                if live(2):
                    p, s = pair(t, at - 2)
                    vec.wait_ge(s_rowinv1, p + 1)
                    last = vec.tensor_tensor(trans[:, s], alpha[:, s], rowinv1[:, s].unsqueeze(2).broadcast_to([P, G, N]), ALU.mult)
                    last.then_inc(s_trans, 1)
                if live(0):
                    p, s = pair(t, at - 0)
                    vec.wait_ge(s_load_x[s], loads(t, at - 0))
                    for j in range(G):
                        last = vec.bn_stats(stats0[:, s, j], x0[:, s, j])
                    last.then_inc(s_stat0, 1)
                if live(0):
                    p, s = pair(t, at - 0)
                    vec.wait_ge(s_stat0, p + 1)
                if live(3):
                    p, s = pair(t, at - 3)
                    vec.wait_ge(s_wh1row, p + 1)
                    for j in range(G):
                        last = vec.scalar_tensor_tensor(z2[:, s, j], wh1row[:, N * j:N * (j + 1)], wh_sb[:, s, j, D + 1:D + 2],
                                                        penalty[:, s, j], ALU.add, ALU.add)
                    last.then_inc(s_z2, 1)
                if live(0):
                    p, s = pair(t, at - 0)
                    for j in range(G):
                        last = vec.bn_aggr(moments0[:, s, j], stats0[:, s, j])
                    last.then_inc(s_aggr0, 1)
                if live(3):
                    p, s = pair(t, at - 3)
                    vec.wait_ge(s_z2, p + 1)
                    last = vec.scalar_tensor_tensor(leaky2[:, s], z2[:, s], SLOPE, z2[:, s], ALU.mult, ALU.max)
                    last.then_inc(s_leaky2, 1)
                if live(1):
                    p, s = pair(t, at - 1)
                    vec.wait_ge(s_mix0, p + 1)
                    last = vec.reciprocal(rowinv0[:, s], mix0[:, :, D + 1])
                    last.then_inc(s_rowinv0, 1)
                if live(0):
                    p, s = pair(t, at - 0)
                    vec.wait_ge(s_aggr0, p + 1)
                    vec.tensor_scalar(negmean0[:, s], moments0[:, s, :, 0], -1.0, None, ALU.mult)
                    last = vec.tensor_scalar(vareps0[:, s], moments0[:, s, :, 1], LN_EPS, None, ALU.add)
                    last.then_inc(s_mom0, 1)
                if live(3):
                    p, s = pair(t, at - 3)
                    vec.wait_ge(s_leaky2, p + 1)
                    last = vec.tensor_reduce(max2[:, s], leaky2[:, s], AX.X, ALU.max)
                    last.then_inc(s_max2, 1)
                if live(3):
                    p, s = pair(t, at - 3)
                    vec.wait_ge(s_max2, p + 1)
                    last = vec.tensor_scalar(negmax2[:, s], max2[:, s], -1.0, None, ALU.mult)
                    last.then_inc(s_negmax2, 1)
                if live(1):
                    p, s = pair(t, at - 1)
                    vec.wait_ge(s_rowinv0, p + 1)
                    vec.wait_ge(s_xb, p + 1)
                    for j in range(G):
                        last = vec.scalar_tensor_tensor(x1[:, s, j], mix0[:, j, 0:D], rowinv0[:, s, j:j + 1], xb[:, s, j],
                                                        ALU.mult, ALU.add)
                    last.then_inc(s_x1, 1)
                if live(1):
                    p, s = pair(t, at - 1)
                    vec.wait_ge(s_x1, p + 1)
                    for j in range(G):
                        last = vec.bn_stats(stats1[:, s, j], x1[:, s, j])
                    last.then_inc(s_stat1, 1)
                if live(3):
                    p, s = pair(t, at - 3)
                    vec.wait_ge(s_exp2, p + 1)
                    last = vec.reciprocal(suminv2[:, s], sum2[:, s])
                    last.then_inc(s_suminv2, 1)
                if live(1):
                    p, s = pair(t, at - 1)
                    count = held(vec, p + 1)
                    vec.wait_ge(s_setup_v, SETUP_STEPS)
                    vec.wait_ge(s_stat1, count)
                    for j in range(G):
                        last = vec.bn_aggr(moments1[:, s, j], stats1[:, s, j])
                    last.then_inc(s_aggr1, 1)
                if live(3):
                    p, s = pair(t, at - 3)
                    vec.wait_ge(s_suminv2, p + 1)
                    last = vec.tensor_tensor(att2[:, s], exp2[:, s], suminv2[:, s].unsqueeze(2).broadcast_to([P, G, N]), ALU.mult)
                    last.then_inc(s_att2, 1)
                if live(1):
                    p, s = pair(t, at - 1)
                    vec.wait_ge(s_aggr1, p + 1)
                    vec.tensor_scalar(negmean1[:, s], moments1[:, s, :, 0], -1.0, None, ALU.mult)
                    last = vec.tensor_scalar(vareps1[:, s], moments1[:, s, :, 1], LN_EPS, None, ALU.add)
                    last.then_inc(s_mom1, 1)
                if live(4):
                    p, s = pair(t, at - 4)
                    vec.wait_ge(s_adjk, p + 1)
                    for j in range(G):
                        last = vec.scalar_tensor_tensor(w3_prod[:, s, j], adjk[:, j, :], INV_SCALE, vqk_sb[:, s, j, D:D + ATT],
                                                        ALU.mult, ALU.mult, accum_out=w3[:, s, j:j + 1])
                    last.then_inc(s_w3, 1)
                if live(4):
                    p, s = pair(t, at - 4)
                    vec.wait_ge(s_w3row, p + 1)
                    last = vec.tensor_reduce(max3[:, s], w3row, AX.X, ALU.max)
                    last.then_inc(s_max3, 1)
                if live(0):
                    p, s = pair(t, at - 0)
                    vec.wait_ge(s_h0, p + 1)
                    last = vec.tensor_copy(h_hi0[:, s], h0[:, s])
                    last.then_inc(s_hi0, 1)
                if live(3):
                    p, s = pair(t, at - 3)
                    vec.wait_ge(s_elu_exp, p + 1)
                    vec.wait_ge(s_mix2, p + 1)
                    last = vec.scalar_tensor_tensor(elu_pos[:, s], mix2, 0.0, x2[:, s], ALU.max, ALU.add)
                    last.then_inc(s_elu_pos, 1)
                if live(4):
                    p, s = pair(t, at - 4)
                    vec.wait_ge(s_max3, p + 1)
                    last = vec.tensor_scalar(negmax3[:, s], max3[:, s], -1.0, None, ALU.mult)
                    last.then_inc(s_negmax3, 1)
                if live(3):
                    p, s = pair(t, at - 3)
                    vec.wait_ge(s_elu_pos, p + 1)
                    last = vec.scalar_tensor_tensor(x3[:, s], elu_exp[:, s], 1.0, elu_pos[:, s], ALU.min, ALU.add)
                    last.then_inc(s_x3, 1)
                if live(1):
                    p, s = pair(t, at - 1)
                    vec.wait_ge(s_hi1, p + 1)
                    vec.wait_ge(s_turn1, p + 1)
                    last = vec.scalar_tensor_tensor(h_lo1[:, s], turn1, 0.0, h_hi1[:, s].bitcast(F32), ALU.max, ALU.subtract)
                    last.then_inc(s_lo1, 1)
                if live(2):
                    p, s = pair(t, at - 2)
                    vec.wait_ge(s_hop0_0, p + 1)
                    last = vec.scalar_tensor_tensor(x2[:, s], hop0, 0.0, x1[:, s], ALU.max, ALU.add)
                    last.then_inc(s_x2, 1)
                if live(4):
                    p, s = pair(t, at - 4)
                    vec.wait_ge(s_exp3, p + 1)
                    last = vec.reciprocal(suminv3[:, s], sum3[:, s])
                    last.then_inc(s_suminv3, 1)
                if live(2):
                    p, s = pair(t, at - 2)
                    vec.wait_ge(s_x2, p + 1)
                    for j in range(G):
                        last = vec.bn_stats(stats2[:, s, j], x2[:, s, j])
                    last.then_inc(s_stat2, 1)
                if live(2):
                    p, s = pair(t, at - 2)
                    count = held(vec, p + 1)
                    vec.wait_ge(s_setup_v, SETUP_STEPS)
                    vec.wait_ge(s_stat2, count)
                    for j in range(G):
                        last = vec.bn_aggr(moments2[:, s, j], stats2[:, s, j])
                    last.then_inc(s_aggr2, 1)
                if live(2):
                    p, s = pair(t, at - 2)
                    vec.wait_ge(s_aggr2, p + 1)
                    vec.tensor_scalar(negmean2[:, s], moments2[:, s, :, 0], -1.0, None, ALU.mult)
                    last = vec.tensor_scalar(vareps2[:, s], moments2[:, s, :, 1], LN_EPS, None, ALU.add)
                    last.then_inc(s_mom2, 1)
                if live(3):
                    p, s = pair(t, at - 3)
                    vec.wait_ge(s_x3, p + 1)
                    for j in range(G):
                        last = vec.bn_stats(stats3[:, s, j], x3[:, s, j])
                    last.then_inc(s_stat3, 1)
                if live(3):
                    p, s = pair(t, at - 3)
                    count = held(vec, p + 1)
                    vec.wait_ge(s_setup_v, SETUP_STEPS)
                    vec.wait_ge(s_stat3, count)
                    for j in range(G):
                        last = vec.bn_aggr(moments3[:, s, j], stats3[:, s, j])
                    last.then_inc(s_aggr3, 1)
                if live(2):
                    p, s = pair(t, at - 2)
                    vec.wait_ge(s_load_adjT2[s], loads(t, at - 2))
                    last = vec.tensor_scalar(penalty[:, s], adjT2[:, s], 0.5, MASKED_Z, ALU.is_le, ALU.mult)
                if live(1):
                    p, s = pair(t, at - 1)
                    vec.wait_ge(s_hop2_out, p + 1)
                    last = vec.tensor_tensor(sij[:, s], hop2_sb[:, s, :, D:D + 2], sij_const[:, :, :], ALU.add)
                    last.then_inc(s_sij, 1)
                if live(3):
                    p, s = pair(t, at - 3)
                    vec.wait_ge(s_aggr3, p + 1)
                    vec.tensor_scalar(negmean3[:, s], moments3[:, s, :, 0], -1.0, None, ALU.mult)
                    last = vec.tensor_scalar(vareps3[:, s], moments3[:, s, :, 1], LN_EPS, None, ALU.add)
                    last.then_inc(s_mom3, 1)
                if live(4):
                    p, s = pair(t, at - 4)
                    vec.wait_ge(s_suminv3, p + 1)
                    last = vec.tensor_scalar(soft3[:, s], exp3[:, s], suminv3[:, s], None, ALU.mult)
                    last.then_inc(s_soft3, 1)
                if live(0):
                    p, s = pair(t, at - 0)
                    vec.wait_ge(s_val0_out, p + 1)
                    last = vec.tensor_scalar(kbias[:, s], val0_sb[:, s, :, D], qk_const[:, 0:1], None, ALU.add)
                    last.then_inc(s_kbias, 1)
                if live(4):
                    p, s = pair(t, at - 4)
                    vec.wait_ge(s_w3col_out, p + 1)
                    if exists(p - 2):
                        vec.wait_ge(s_store[s], loads(t, at - 4 - 2))
                    for j in range(G):
                        last = vec.scalar_tensor_tensor(y[:, s, j], vqk_sb[:, s, j, 0:D], w3col_sb[:, s, j:j + 1], x3[:, s, j],
                                                        ALU.mult, ALU.add)
                    last.then_inc(s_out, 1)
                if live(2):
                    p, s = pair(t, at - 2)
                    vec.wait_ge(s_hi2, p + 1)
                    vec.wait_ge(s_turn2, p + 1)
                    last = vec.scalar_tensor_tensor(h_lo2[:, s], turn2, 0.0, h_hi2[:, s].bitcast(F32), ALU.max, ALU.subtract)
                    last.then_inc(s_lo2, 1)

            run(vec, step)


def kernel(**inputs):
    import numpy as np
    import concourse.bacc as bacc
    from concourse.bass_utils import run_bass_kernel_spmd

    a = {name: np.asarray(value) for name, value in inputs.items()}
    graphs, nodes, features = a["x"].shape

    def by_pair(v):
        return np.ascontiguousarray(v.reshape(graphs // G, G, nodes, -1).transpose(0, 2, 1, 3))

    def by_half(v):
        return np.ascontiguousarray(v.reshape(features // P, P, -1).transpose(1, 0, 2))

    zeros = np.zeros((features, 2), np.float32)
    weights = np.concatenate([
        a["L0_gnn_Wv_w"].T, zeros, a["L1_gnn_Wk"][2], zeros, a["L2_gnn_W"], zeros, a["L1_gnn_Wk"][1],
        a["L1_gnn_Wk"][0], a["L3_gnn_W_v"].T, a["L3_gnn_W_qk"].T, np.zeros((features, features), np.float32)], 1)
    aw, ag = a["L1_gnn_aw"].reshape(2, features), a["L2_gnn_a"].reshape(2, features)
    setup = np.concatenate([
        a["L0_gnn_Wk_w"], a["L0_gnn_Wq_w"], a["L0_gnn_Wq_b"][:, None], a["L0_gnn_Wk_b"][:, None],
        a["L1_gnn_Wv"].T, aw[::-1].T, a["L1_gnn_bv"][:, None], a["L2_gnn_W"].T, ag.T], 1)
    arrays = {
        "x_in": by_pair(a["x"]), "adj_in": by_pair(a["adj"]), "adjT_in": by_pair(a["adj"].transpose(0, 2, 1)),
        "weights_in": by_half(weights), "setup_in": by_half(setup), "hop_bias_in": a["L1_gnn_bk"],
        "value_bias_in": a["L0_gnn_Wv_b"], "ab_in": a["L1_gnn_ab"]}
    nc = bacc.Bacc("TRN2", target_bir_lowering=False, num_devices=1)
    args = [nc.dram_tensor(name, v.shape, F32, kind="ExternalInput").ap() for name, v in arrays.items()]
    y = nc.dram_tensor("y_out", arrays["x_in"].shape, F32, kind="ExternalOutput").ap()
    graph_layers_kernel(nc, *args, y)
    result = run_bass_kernel_spmd(nc, [arrays], core_ids=[0]).results[0]["y_out"]
    return np.asarray(result).transpose(0, 2, 1, 3).reshape(graphs, nodes, features)
```

```python
from contextlib import ExitStack

import concourse.bass as bass
from concourse import mybir

ALU = mybir.AluOpType
ACT = mybir.ActivationFunctionType
AX = mybir.AxisListType
F32 = mybir.dt.float32
F32R = mybir.dt.float32r

P = 128
LN_EPS = 1e-5
ROWSUM_EPS = 1e-12
SLOPE = 0.2
MASKED = -9e15
MASKED_Z = MASKED / SLOPE
G = 2
PAIRS = 32
STAGES = 4

D_ = 256
KQ, KB, V0 = 0, 256, 257
HOP2, HOP1, HOP0 = 514, 772, 1028
WH, VQK, W_COLS = 1284, 1542, 1926
S_WK, S_WQ, S_BQ, S_BK, S_WV1, S_A1, S_BV1, S_WG, S_AG = 0, 256, 512, 513, 514, 770, 772, 773, 1029
S_COLS = 1031


def pair(t, at):
    return 2 * t + at, at % 2


def exists(p):
    return not isinstance(p, int) or p >= 0


def first(p):
    return isinstance(p, int) and p == 0


def upto(count):
    return min(count, PAIRS) if isinstance(count, int) else count


def held(eng, count):
    return count if isinstance(count, int) else eng.snap(count)


def loads(t, at):
    return 16 * (t + at // 2) + 16


def split_product(pe, out, stationary, stationary_parts, moving, moving_parts, stop=True):
    (s_hi, s_lo), (m_hi, m_lo) = stationary_parts, moving_parts
    terms = ((s_hi, m_hi), (s_hi, m_lo), (s_lo, m_hi))
    for c in range(2):
        for n, (a, b) in enumerate(terms):
            last = pe.matmul(out, stationary(a, c), moving(b, c), start=(c == 0 and n == 0),
                             stop=(stop and c == 1 and n == 2))
    return last


def graph_layers_kernel(nc: bass.Bass, x_in, adj_in, adjT_in, weights_in, setup_in, hop_bias_in, value_bias_in,
                        ab_in, y_out):
    pairs, N, _, D = x_in.shape
    assert pairs == PAIRS and N == P and D == D_
    C = D // P
    ATT = 64
    QK = 2 * ATT
    INV_SCALE = ATT ** -0.5

    with ExitStack() as ctx:
        def sb(name, *shape, dt=F32):
            return ctx.enter_context(nc.sbuf_tensor(name, [P, *shape], dt))

        def sem(name):
            return ctx.enter_context(nc.semaphore(name))

        ident = sb("ident", P)
        minus_half = sb("minus_half", G)
        ones_r = sb("ones_r", P, dt=F32R)
        w_all = sb("w_all", C, W_COLS)
        w_hi = sb("w_hi", C, W_COLS, dt=F32R)
        w_lo = sb("w_lo", C, W_COLS, dt=F32R)
        w_setup = sb("w_setup", C, S_COLS)
        hop_rows = sb("hop_rows", D)
        hop_rows_hi = sb("hop_rows_hi", D, dt=F32R)
        hop_bias = sb("hop_bias", D, dt=F32R)
        value_row = sb("value_row", D)
        value_bias = sb("value_bias", G, D)
        ab_col = sb("ab_col", 1)
        vectors = sb("vectors", 13)
        sij_const = sb("sij_const", G, 2)

        def parts(start, width):
            return w_hi[:, :, start:start + width], w_lo[:, :, start:start + width]

        w_v0, w_hop2, w_wh = parts(KB, D + 2), parts(HOP2, D + 2), parts(WH, D + 2)
        w_hop1, w_hop0, w_vqk, w_kq = parts(HOP1, D), parts(HOP0, D), parts(VQK, D + QK), parts(KQ, D)

        x0, x1, x2, x3, y, xb = (sb(n, 2, G, D) for n in ("x0", "x1", "x2", "x3", "y", "xb"))
        adjT0, adj1, adjT2 = (sb(n, 2, G, N) for n in ("adjT0", "adj1", "adjT2"))
        stats0, stats1, stats2, stats3 = (sb(f"stats{n}", 2, G, 6) for n in range(4))
        moments0, moments1, moments2, moments3 = (sb(f"moments{n}", 2, G, 2) for n in range(4))
        negmean0, negmean1, negmean2, negmean3 = (sb(f"negmean{n}", 2, G) for n in range(4))
        vareps0, vareps1, vareps2, vareps3 = (sb(f"vareps{n}", 2, G) for n in range(4))
        rstd0, rstd1, rstd2, rstd3 = (sb(f"rstd{n}", 2, G) for n in range(4))
        normed0, normed1, normed2, normed3 = (sb(f"normed{n}", 2, G, D) for n in range(4))
        h0 = sb("h0", 2, C, G * N)
        h_hi0, h_hi1, h_hi2, h_hi3 = (sb(f"h_hi{n}", 2, C, G * N, dt=F32R) for n in range(4))
        h_lo0, h_lo1, h_lo2, h_lo3 = (sb(f"h_lo{n}", 2, C, G * N, dt=F32R) for n in range(4))
        keyq_sb = sb("keyq_sb", 2, C, G * N)
        val0_sb = sb("val0_sb", 2, G, D + 2)
        kbias, rowinv0 = sb("kbias", 2, G), sb("rowinv0", 2, G)
        exp0, att0 = sb("exp0", 2, G, N), sb("att0", 2, G, N)
        hop2_sb, hop1_sb = sb("hop2_sb", 2, G, D + 2), sb("hop1_sb", 2, G, D)
        sij = sb("sij", 2, G, 2)
        z1, leaky1, exp1, alpha, trans = (sb(n, 2, G, N) for n in ("z1", "leaky1", "exp1", "alpha", "trans"))
        rowsum1, rowsum1e, rowinv1 = (sb(n, 2, G) for n in ("rowsum1", "rowsum1e", "rowinv1"))
        transT_sb = sb("transT_sb", 2, G * N)
        wh_sb = sb("wh_sb", 2, G, D + 2)
        penalty, z2, leaky2, exp2, att2 = (sb(n, 2, G, N) for n in ("penalty", "z2", "leaky2", "exp2", "att2"))
        max2, negmax2, sum2, suminv2 = (sb(n, 2, G) for n in ("max2", "negmax2", "sum2", "suminv2"))
        elu_exp, elu_pos = sb("elu_exp", 2, G, D), sb("elu_pos", 2, G, D)
        vqk_sb = sb("vqk_sb", 2, G, D + QK)
        w3_prod, w3, w3col_sb = sb("w3_prod", 2, G, ATT), sb("w3", 2, G), sb("w3col_sb", 2, G)

        def rows(name, width):
            return ctx.enter_context(nc.sbuf_tensor(name, [G, 2, width], F32))

        max3, negmax3, sum3, suminv3 = (rows(n, 1) for n in ("max3", "negmax3", "sum3", "suminv3"))
        exp3, soft3 = rows("exp3", N), rows("soft3", N)

        psum = ctx.enter_context(nc.psum_tensor("psum", [P, 8, 512], F32))
        turn0 = psum[:, 6].rearrange("p (c n) -> p c n", c=C)
        keyq = psum[:, 4].rearrange("p (c n) -> p c n", c=C)
        val0 = psum[:, 5:7]
        score0 = psum[:, 7, 0:G * N]
        mix0 = psum[:, 0:2]
        turn1 = psum[:, 5].rearrange("p (c n) -> p c n", c=C)
        hop2 = psum[:, 4:6]
        sjrow = psum[:, 0, 0:G * N]
        transT = psum[:, 6, 0:G * N]
        hop1 = psum[:, 6].rearrange("p (j d) -> p j d", j=G)
        hop0 = psum[:, 1].rearrange("p (j d) -> p j d", j=G)
        turn2 = psum[:, 1].rearrange("p (c n) -> p c n", c=C)
        wh = psum[:, 3:5]
        wh1row = psum[:, 5, 0:G * N]
        mix2 = psum[:, 2].rearrange("p (j d) -> p j d", j=G)
        turn3 = psum[:, 2].rearrange("p (c n) -> p c n", c=C)
        vqk = psum[:, 3:5]
        adjk = psum[:, 3, 0:G * ATT].rearrange("p (j d) -> p j d", j=G)
        w3row = psum[0:G, 3, 0:N]
        w3col = psum[:, 1, 0:G]

        s_constants = sem("constants")
        s_constants_v = sem("constants_v")
        s_load_bias = sem("load_bias")
        s_load_w0 = sem("load_w0")
        s_load_setup0 = sem("load_setup0")
        s_load_setup1 = sem("load_setup1")
        s_load_hops = sem("load_hops")
        s_load_w1 = sem("load_w1")
        s_load_w2 = sem("load_w2")
        s_products = sem("products")
        s_vectors = sem("vectors")
        s_upper0 = sem("upper0")
        s_upper1 = sem("upper1")
        s_upper2 = sem("upper2")
        s_lower0 = sem("lower0")
        s_lower1 = sem("lower1")
        s_lower2 = sem("lower2")
        s_load_x = [sem(f"load_x_{i}") for i in range(2)]
        s_load_adjT0 = [sem(f"load_adjT0_{i}") for i in range(2)]
        s_stat0 = sem("stat0")
        s_aggr0 = sem("aggr0")
        s_mom0 = sem("mom0")
        s_rstd0 = sem("rstd0")
        s_norm0 = sem("norm0")
        s_turn0 = sem("turn0")
        s_h0 = sem("h0")
        s_hi0 = sem("hi0")
        s_lo0 = sem("lo0")
        s_xb = sem("xb")
        s_keyq = sem("keyq")
        s_keyq_out = sem("keyq_out")
        s_val0 = sem("val0")
        s_val0_out = sem("val0_out")
        s_kbias = sem("kbias")
        s_score0 = sem("score0")
        s_exp0 = sem("exp0")
        s_att0 = sem("att0")
        s_mix0 = sem("mix0")
        s_rowinv0 = sem("rowinv0")
        s_x1 = sem("x1")
        s_load_adj1 = [sem(f"load_adj1_{i}") for i in range(2)]
        s_stat1 = sem("stat1")
        s_aggr1 = sem("aggr1")
        s_mom1 = sem("mom1")
        s_rstd1 = sem("rstd1")
        s_norm1 = sem("norm1")
        s_turn1 = sem("turn1")
        s_hi1 = sem("hi1")
        s_lo1 = sem("lo1")
        s_hop2 = sem("hop2")
        s_hop2_out = sem("hop2_out")
        s_sij = sem("sij")
        s_sjrow = sem("sjrow")
        s_z1 = sem("z1")
        s_leaky1 = sem("leaky1")
        s_exp1 = sem("exp1")
        s_alpha = sem("alpha")
        s_rowsum1e = sem("rowsum1e")
        s_rowinv1 = sem("rowinv1")
        s_trans = sem("trans")
        s_transT = sem("transT")
        s_transT_out = sem("transT_out")
        s_hop1_0 = sem("hop1_0")
        s_hop1_out = sem("hop1_out")
        s_hop0_0 = sem("hop0_0")
        s_x2 = sem("x2")
        s_load_adjT2 = [sem(f"load_adjT2_{i}") for i in range(2)]
        s_stat2 = sem("stat2")
        s_aggr2 = sem("aggr2")
        s_mom2 = sem("mom2")
        s_rstd2 = sem("rstd2")
        s_norm2 = sem("norm2")
        s_turn2 = sem("turn2")
        s_hi2 = sem("hi2")
        s_lo2 = sem("lo2")
        s_penalty = sem("penalty")
        s_wh_out = sem("wh_out")
        s_wh1row = sem("wh1row")
        s_z2 = sem("z2")
        s_leaky2 = sem("leaky2")
        s_max2 = sem("max2")
        s_negmax2 = sem("negmax2")
        s_exp2 = sem("exp2")
        s_suminv2 = sem("suminv2")
        s_att2 = sem("att2")
        s_mix2 = sem("mix2")
        s_elu_exp = sem("elu_exp")
        s_elu_pos = sem("elu_pos")
        s_x3 = sem("x3")
        s_stat3 = sem("stat3")
        s_aggr3 = sem("aggr3")
        s_mom3 = sem("mom3")
        s_rstd3 = sem("rstd3")
        s_norm3 = sem("norm3")
        s_turn3 = sem("turn3")
        s_hi3 = sem("hi3")
        s_lo3 = sem("lo3")
        s_vqk_0 = sem("vqk_0")
        s_vqk_out = sem("vqk_out")
        s_adjk = sem("adjk")
        s_w3 = sem("w3")
        s_w3row = sem("w3row")
        s_max3 = sem("max3")
        s_negmax3 = sem("negmax3")
        s_exp3 = sem("exp3")
        s_suminv3 = sem("suminv3")
        s_soft3 = sem("soft3")
        s_w3col = sem("w3col")
        s_w3col_out = sem("w3col_out")
        s_out = sem("out")
        s_store = [sem(f"store_{i}") for i in range(2)]

        CONSTANTS_V = 6
        keyq_weights = psum[:, 0:0 + C, 0:D + 1]
        small = psum[:, 2]
        block = ctx.enter_context(nc.Block())

        def run(eng, step):
            full_from = (STAGES + 3) // 2
            for k in range(2 * full_from):
                step(0, k, lambda g: 0 <= k - g < PAIRS)
            with eng.Fori(full_from, PAIRS // 2) as t:
                for c in range(2):
                    step(t, c, lambda g: True)
            for k in range(PAIRS, PAIRS + STAGES):
                step(0, k, lambda g: 0 <= k - g < PAIRS)

        @block.sync
        def _(sync):
            sync.dma_start(w_setup[:, :, 0:S_WV1], setup_in[:, :, 0:S_WV1]).then_inc(s_load_setup0, 16)

            def load_w(start, end, loaded):
                sync.dma_start(w_all[:, :, start:end], weights_in[:, :, start - V0:end - V0]).then_inc(loaded, 16)

            def load_weights0():
                sync.dma_start(w_setup[:, :, S_WV1:S_COLS], setup_in[:, :, S_WV1:S_COLS]).then_inc(s_load_setup1, 16)
                load_w(V0, HOP2, s_load_w0)
                sync.dma_start(value_row[:, :], value_bias_in.partition_broadcast(P)).then_inc(s_load_bias, 16)

            def load_weights1():
                load_w(HOP2, WH, s_load_w1)
                sync.dma_start(ab_col[:, :], ab_in.partition_broadcast(P)).then_inc(s_load_hops, 16)
                sync.wait_ge(s_constants, 1)
                for q in (0, 32):
                    sync.dma_start(hop_rows[q:q + 3, :], hop_bias_in).then_inc(s_load_hops, 16)

            def load_weights2():
                load_w(WH, W_COLS, s_load_w2)

            def step(t, at, live):
                if live(0):
                    p, s = pair(t, at - 0)
                    if exists(p - 2):
                        sync.wait_ge(s_xb, p - 1)
                    last = sync.dma_start(x0[:, s], x_in[p])
                    last.then_inc(s_load_x[s], 16)
                if live(0):
                    p, s = pair(t, at - 0)
                    if first(p):
                        load_weights0()
                    if exists(p - 2):
                        sync.wait_ge(s_att0, p - 1)
                    last = sync.dma_start(adjT0[:, s], adjT_in[p])
                    last.then_inc(s_load_adjT0[s], 16)
                if live(2):
                    p, s = pair(t, at - 2)
                    if first(p):
                        load_weights2()
                    if exists(p - 2):
                        sync.wait_ge(s_adjk, p - 1)
                    last = sync.dma_start(adjT2[:, s], adjT_in[p])
                    last.then_inc(s_load_adjT2[s], 16)
                if live(0):
                    p, s = pair(t, at - 0)
                    if first(p):
                        load_weights1()
                    if exists(p - 2):
                        sync.wait_ge(s_alpha, p - 1)
                    last = sync.dma_start(adj1[:, s], adj_in[p])
                    last.then_inc(s_load_adj1[s], 16)
                if live(4):
                    p, s = pair(t, at - 4)
                    sync.wait_ge(s_out, p + 1)
                    last = sync.dma_start(y_out[p], y[:, s])
                    last.then_inc(s_store[s], 16)

            run(sync, step)
            for i in range(2):
                sync.wait_ge(s_store[i], 16 * (PAIRS // 2))

        @block.gpsimd
        def _(pool):
            pool.memset(hop_rows[:, :], 0.0).then_inc(s_constants, 1)
            pool.memset(ident[:, :], 0.0).then_inc(s_constants, 1)
            pool.wait_ge(s_constants, 2)
            pool.affine_select(out=ident[:, :], in_=ident[:, :], compare_op=ALU.not_equal, fill=1.0, base=0,
                               pattern=[[-1, P]], channel_multiplier=1).then_inc(s_constants, 1)
            pool.memset(minus_half[:, :], -0.5).then_inc(s_constants, 1)
            pool.wait_ge(s_constants, 4)

            def step(t, at, live):
                if live(1):
                    p, s = pair(t, at - 1)
                    if first(p):
                        pool.wait_ge(s_constants_v, CONSTANTS_V)
                    last = pool.tensor_tensor(xb[:, s], x0[:, s], value_bias[:, :, :], ALU.add)
                    last.then_inc(s_xb, 1)
                if live(1):
                    p, s = pair(t, at - 1)
                    pool.wait_ge(s_mom1, p + 1)
                    last = pool.tensor_tensor(rstd1[:, s], vareps1[:, s], minus_half[:, :], ALU.pow)
                    last.then_inc(s_rstd1, 1)
                if live(1):
                    p, s = pair(t, at - 1)
                    count = held(pool, p + 1)
                    pool.wait_ge(s_constants, 4)
                    pool.wait_ge(s_rstd1, count)
                    for j in range(G):
                        last = pool.tensor_scalar(normed1[:, s, j], x1[:, s, j], negmean1[:, s, j:j + 1],
                                                  rstd1[:, s, j:j + 1], ALU.add, ALU.mult)
                    last.then_inc(s_norm1, 1)
                if live(0):
                    p, s = pair(t, at - 0)
                    pool.wait_ge(s_mom0, p + 1)
                    last = pool.tensor_tensor(rstd0[:, s], vareps0[:, s], minus_half[:, :], ALU.pow)
                    last.then_inc(s_rstd0, 1)
                if live(0):
                    p, s = pair(t, at - 0)
                    count = held(pool, p + 1)
                    pool.wait_ge(s_constants, 4)
                    pool.wait_ge(s_rstd0, count)
                    for j in range(G):
                        last = pool.tensor_scalar(normed0[:, s, j], x0[:, s, j], negmean0[:, s, j:j + 1],
                                                  rstd0[:, s, j:j + 1], ALU.add, ALU.mult)
                    last.then_inc(s_norm0, 1)
                if live(0):
                    p, s = pair(t, at - 0)
                    pool.wait_ge(s_hi0, p + 1)
                    last = pool.tensor_tensor(h_lo0[:, s], h0[:, s], h_hi0[:, s].bitcast(F32), ALU.subtract)
                    last.then_inc(s_lo0, 1)
                if live(2):
                    p, s = pair(t, at - 2)
                    pool.wait_ge(s_mom2, p + 1)
                    last = pool.tensor_tensor(rstd2[:, s], vareps2[:, s], minus_half[:, :], ALU.pow)
                    last.then_inc(s_rstd2, 1)
                if live(2):
                    p, s = pair(t, at - 2)
                    count = held(pool, p + 1)
                    pool.wait_ge(s_constants, 4)
                    pool.wait_ge(s_rstd2, count)
                    for j in range(G):
                        last = pool.tensor_scalar(normed2[:, s, j], x2[:, s, j], negmean2[:, s, j:j + 1],
                                                  rstd2[:, s, j:j + 1], ALU.add, ALU.mult)
                    last.then_inc(s_norm2, 1)
                if live(3):
                    p, s = pair(t, at - 3)
                    pool.wait_ge(s_mom3, p + 1)
                    last = pool.tensor_tensor(rstd3[:, s], vareps3[:, s], minus_half[:, :], ALU.pow)
                    last.then_inc(s_rstd3, 1)
                if live(3):
                    p, s = pair(t, at - 3)
                    count = held(pool, p + 1)
                    pool.wait_ge(s_constants, 4)
                    pool.wait_ge(s_rstd3, count)
                    for j in range(G):
                        last = pool.tensor_scalar(normed3[:, s, j], x3[:, s, j], negmean3[:, s, j:j + 1],
                                                  rstd3[:, s, j:j + 1], ALU.add, ALU.mult)
                    last.then_inc(s_norm3, 1)

            run(pool, step)

        @block.scalar
        def _(act):
            def split_upper0():
                act.wait_ge(s_products, 1)
                act.activation(w_hi[:, :, KQ:KB + 1], keyq_weights, ACT.Copy).then_inc(s_upper0, 1)
                act.wait_ge(s_load_w0, 16)
                act.activation(w_hi[:, :, V0:HOP2], w_all[:, :, V0:HOP2], ACT.Copy).then_inc(s_upper0, 1)

            def split_upper1():
                act.wait_ge(s_load_w1, 16)
                act.wait_ge(s_vectors, 2)
                act.activation(w_hi[:, :, HOP2:WH], w_all[:, :, HOP2:WH], ACT.Copy).then_inc(s_upper1, 1)

            def split_upper2():
                act.wait_ge(s_load_w2, 16)
                act.wait_ge(s_vectors, 7)
                act.activation(w_hi[:, :, WH:W_COLS], w_all[:, :, WH:W_COLS], ACT.Copy).then_inc(s_upper2, 1)

            def step(t, at, live):
                if live(3):
                    p, s = pair(t, at - 3)
                    last = act.activation(wh_sb[:, s], wh[:, :, 0:D + 2], ACT.Copy)
                    last.then_inc(s_wh_out, 1)
                if live(4):
                    p, s = pair(t, at - 4)
                    act.wait_ge(s_turn3, p + 1)
                    last = act.activation(h_hi3[:, s], turn3, ACT.Relu)
                    last.then_inc(s_hi3, 1)
                if live(2):
                    p, s = pair(t, at - 2)
                    act.wait_ge(s_hop1_0, p + 1)
                    last = act.activation(hop1_sb[:, s], hop1, ACT.Copy)
                    last.then_inc(s_hop1_out, 1)
                if live(3):
                    p, s = pair(t, at - 3)
                    act.wait_ge(s_negmax2, p + 1)
                    for j in range(G):
                        last = act.activation(exp2[:, s, j], leaky2[:, s, j], ACT.Exp, bias=negmax2[:, s, j:j + 1],
                                              accum_out=sum2[:, s, j:j + 1])
                    last.then_inc(s_exp2, 1)
                if live(1):
                    p, s = pair(t, at - 1)
                    act.wait_ge(s_turn1, p + 1)
                    last = act.activation(h_hi1[:, s], turn1, ACT.Relu)
                    last.then_inc(s_hi1, 1)
                if live(4):
                    p, s = pair(t, at - 4)
                    act.wait_ge(s_vqk_0, p + 1)
                    last = act.activation(vqk_sb[:, s], vqk[:, :, 0:D + QK], ACT.Copy)
                    last.then_inc(s_vqk_out, 1)
                if live(0):
                    p, s = pair(t, at - 0)
                    if first(p):
                        split_upper0()
                    act.wait_ge(s_turn0, p + 1)
                    last = act.activation(h0[:, s], turn0, ACT.Relu)
                    last.then_inc(s_h0, 1)
                if live(1):
                    p, s = pair(t, at - 1)
                    if first(p):
                        split_upper2()
                    act.wait_ge(s_hop2, p + 1)
                    last = act.activation(hop2_sb[:, s], hop2[:, :, 0:D + 2], ACT.Copy)
                    last.then_inc(s_hop2_out, 1)
                if live(3):
                    p, s = pair(t, at - 3)
                    act.wait_ge(s_mix2, p + 1)
                    last = act.activation(elu_exp[:, s], mix2, ACT.Exp)
                    last.then_inc(s_elu_exp, 1)
                if live(1):
                    p, s = pair(t, at - 1)
                    act.wait_ge(s_sij, p + 1)
                    act.wait_ge(s_sjrow, p + 1)
                    for j in range(G):
                        last = act.activation(z1[:, s, j], sjrow[:, N * j:N * (j + 1)], ACT.Identity, bias=sij[:, s, j, 0:1])
                    last.then_inc(s_z1, 1)
                if live(0):
                    p, s = pair(t, at - 0)
                    if first(p):
                        split_upper1()
                    act.wait_ge(s_keyq, p + 1)
                    for m in range(C):
                        last = act.activation(keyq_sb[:, s, m, :], keyq[:, m, :], ACT.Identity, bias=vectors[:, m:m + 1])
                    last.then_inc(s_keyq_out, 1)
                if live(1):
                    p, s = pair(t, at - 1)
                    act.wait_ge(s_leaky1, p + 1)
                    last = act.activation(exp1[:, s], leaky1[:, s], ACT.Exp)
                    last.then_inc(s_exp1, 1)
                if live(2):
                    p, s = pair(t, at - 2)
                    act.wait_ge(s_turn2, p + 1)
                    last = act.activation(h_hi2[:, s], turn2, ACT.Relu)
                    last.then_inc(s_hi2, 1)
                if live(4):
                    p, s = pair(t, at - 4)
                    act.wait_ge(s_negmax3, p + 1)
                    last = act.activation(exp3[:, s], w3row, ACT.Exp, bias=negmax3[:, s], accum_out=sum3[:, s])
                    last.then_inc(s_exp3, 1)
                if live(0):
                    p, s = pair(t, at - 0)
                    act.wait_ge(s_val0, p + 1)
                    last = act.activation(val0_sb[:, s, :, 0:1 + D], val0[:, :, 0:1 + D], ACT.Copy)
                    last.then_inc(s_val0_out, 1)
                if live(0):
                    p, s = pair(t, at - 0)
                    act.wait_ge(s_kbias, p + 1)
                    act.wait_ge(s_score0, p + 1)
                    for j in range(G):
                        last = act.activation(exp0[:, s, j], score0[:, N * j:N * (j + 1)], ACT.Exp, bias=kbias[:, s, j:j + 1])
                    last.then_inc(s_exp0, 1)
                if live(4):
                    p, s = pair(t, at - 4)
                    act.wait_ge(s_w3col, p + 1)
                    last = act.activation(w3col_sb[:, s], w3col, ACT.Copy)
                    last.then_inc(s_w3col_out, 1)
                if live(1):
                    p, s = pair(t, at - 1)
                    act.wait_ge(s_transT, p + 1)
                    last = act.activation(transT_sb[:, s], transT, ACT.Copy)
                    last.then_inc(s_transT_out, 1)

            run(act, step)

        @block.tensor
        def _(pe):
            pe.wait_ge(s_load_setup0, 16)
            for m in range(C):
                for c in range(C):
                    pe.matmul(keyq_weights[:, m], w_setup[:, c, S_WK + P * m:S_WK + P * (m + 1)],
                              w_setup[:, c, S_WQ:S_WQ + D + 1], start=(c == 0), stop=(c == C - 1))
            for m in range(C):
                for c in range(C):
                    pe.matmul(small[:, m:m + 1], w_setup[:, c, S_WQ + P * m:S_WQ + P * (m + 1)],
                              w_setup[:, c, S_BK:S_BK + 1], start=(c == 0), stop=(c == C - 1))
            for c in range(C):
                pe.matmul(small[:, 2:3], w_setup[:, c, S_BK:S_BK + 1].broadcast_to([P, P]),
                          w_setup[:, c, S_BQ:S_BQ + 1], start=(c == 0), stop=(c == C - 1))
            pe.wait_ge(s_load_setup1, 16)
            for c in range(C):
                pe.matmul(small[:, 3:5], w_setup[:, c, S_BV1:S_BV1 + 1].broadcast_to([P, P]),
                          w_setup[:, c, S_A1:S_A1 + 2], start=(c == 0), stop=(c == C - 1))
            for m in range(C):
                for start, vectors, to in ((S_WV1, S_A1, 5), (S_WG, S_AG, 9)):
                    for c in range(C):
                        last = pe.matmul(small[:, to + 2 * m:to + 2 * m + 2],
                                         w_setup[:, c, start + P * m:start + P * (m + 1)],
                                         w_setup[:, c, vectors:vectors + 2], start=(c == 0), stop=(c == C - 1))
            last.then_inc(s_products, 1)
            pe.wait_ge(s_constants, 3)
            pe.wait_ge(s_constants_v, CONSTANTS_V)

            def step(t, at, live):
                if live(1):
                    p, s = pair(t, at - 1)
                    pe.wait_ge(s_att0, p + 1)
                    if exists(p - 4):
                        pe.wait_ge(s_w3col_out, p - 3)
                    for j in range(G):
                        last = pe.matmul(mix0[:, j, 0:D + 1], att0[:, s, j], val0_sb[:, s, j, 1:D + 2], start=True, stop=True)
                    last.then_inc(s_mix0, 1)
                if live(2):
                    p, s = pair(t, at - 2)
                    pe.wait_ge(s_transT_out, p + 1)
                    split_product(pe, hop1[:, 1, :], lambda h, c: h[:, s, c, N * 1:N * 2], (h_hi1, h_lo1),
                                  lambda w, c: w[:, c, :], w_hop1, stop=False)
                    last = pe.matmul(hop1[:, 1, :], transT_sb[:, s, N * 1:N * 2], hop2_sb[:, s, 1, 0:D], start=False, stop=True)
                if live(3):
                    p, s = pair(t, at - 3)
                    pe.wait_ge(s_wh_out, p + 1)
                    for j in range(G):
                        last = pe.transpose(wh1row[:, N * j:N * (j + 1)], wh_sb[:, s, j, D:D + 1].broadcast_to([N, P]), ident[:, :])
                    last.then_inc(s_wh1row, 1)
                if live(2):
                    p, s = pair(t, at - 2)
                    split_product(pe, hop1[:, 0, :], lambda h, c: h[:, s, c, N * 0:N * 1], (h_hi1, h_lo1),
                                  lambda w, c: w[:, c, :], w_hop1, stop=False)
                    last = pe.matmul(hop1[:, 0, :], transT_sb[:, s, N * 0:N * 1], hop2_sb[:, s, 0, 0:D], start=False, stop=True)
                    last.then_inc(s_hop1_0, 1)
                if live(4):
                    p, s = pair(t, at - 4)
                    pe.wait_ge(s_lo3, p + 1)
                    last = split_product(pe, vqk[:, 1, 0:D + QK], lambda h, c: h[:, s, c, N * 1:N * 2], (h_hi3, h_lo3),
                                         lambda w, c: w[:, c, :], w_vqk)
                if live(4):
                    p, s = pair(t, at - 4)
                    last = split_product(pe, vqk[:, 0, 0:D + QK], lambda h, c: h[:, s, c, N * 0:N * 1], (h_hi3, h_lo3),
                                         lambda w, c: w[:, c, :], w_vqk)
                    last.then_inc(s_vqk_0, 1)
                if live(2):
                    p, s = pair(t, at - 2)
                    pe.wait_ge(s_x1, upto(p + 2))
                    pe.wait_ge(s_hop1_out, p + 1)
                    split_product(pe, hop0[:, 1, :], lambda h, c: h[:, s, c, N * 1:N * 2], (h_hi1, h_lo1),
                                  lambda w, c: w[:, c, :], w_hop0, stop=False)
                    pe.matmul(hop0[:, 1, :], ones_r[:, :], hop_bias[:, :], start=False, stop=False)
                    last = pe.matmul(hop0[:, 1, :], transT_sb[:, s, N * 1:N * 2], hop1_sb[:, s, 1], start=False, stop=True)
                if live(1):
                    p, s = pair(t, at - 1)
                    pe.wait_ge(s_norm1, p + 1)
                    if exists(p - 2):
                        pe.wait_ge(s_z2, p - 1)
                    for j in range(G):
                        for c in range(C):
                            last = pe.transpose(turn1[:, c, N * j:N * (j + 1)], normed1[:, s, j, P * c:P * (c + 1)],
                                                ident[:, :])
                    last.then_inc(s_turn1, 1)
                if live(2):
                    p, s = pair(t, at - 2)
                    split_product(pe, hop0[:, 0, :], lambda h, c: h[:, s, c, N * 0:N * 1], (h_hi1, h_lo1),
                                  lambda w, c: w[:, c, :], w_hop0, stop=False)
                    pe.matmul(hop0[:, 0, :], ones_r[:, :], hop_bias[:, :], start=False, stop=False)
                    last = pe.matmul(hop0[:, 0, :], transT_sb[:, s, N * 0:N * 1], hop1_sb[:, s, 0], start=False, stop=True)
                    last.then_inc(s_hop0_0, 1)
                if live(0):
                    p, s = pair(t, at - 0)
                    pe.wait_ge(s_norm0, p + 1)
                    for j in range(G):
                        for c in range(C):
                            last = pe.transpose(turn0[:, c, N * j:N * (j + 1)], normed0[:, s, j, P * c:P * (c + 1)],
                                                ident[:, :])
                    last.then_inc(s_turn0, 1)
                if live(1):
                    p, s = pair(t, at - 1)
                    if first(p):
                        pe.wait_ge(s_lower1, 4)
                    pe.wait_ge(s_lo1, p + 1)
                    if exists(p - 3):
                        pe.wait_ge(s_vqk_out, p - 2)
                    for j in range(G):
                        last = split_product(pe, hop2[:, j, 0:D + 2], lambda h, c: h[:, s, c, N * j:N * (j + 1)], (h_hi1, h_lo1),
                                             lambda w, c: w[:, c, :], w_hop2)
                    last.then_inc(s_hop2, 1)
                if live(3):
                    p, s = pair(t, at - 3)
                    pe.wait_ge(s_att2, p + 1)
                    for j in range(G):
                        last = pe.matmul(mix2[:, j, :], att2[:, s, j], wh_sb[:, s, j, 0:D], start=True, stop=True)
                    last.then_inc(s_mix2, 1)
                if live(4):
                    p, s = pair(t, at - 4)
                    pe.wait_ge(s_vqk_out, p + 1)
                    for j in range(G):
                        last = pe.matmul(adjk[:, j, :], adjT2[:, s, j], vqk_sb[:, s, j, D + ATT:D + 2 * ATT], start=True, stop=True)
                    last.then_inc(s_adjk, 1)
                if live(1):
                    p, s = pair(t, at - 1)
                    pe.wait_ge(s_sij, p + 1)
                    for j in range(G):
                        last = pe.transpose(sjrow[:, N * j:N * (j + 1)], sij[:, s, j, 1:2].broadcast_to([N, P]), ident[:, :])
                    last.then_inc(s_sjrow, 1)
                if live(0):
                    p, s = pair(t, at - 0)
                    if first(p):
                        pe.wait_ge(s_lower0, 2)
                    pe.wait_ge(s_hi0, p + 1)
                    pe.wait_ge(s_lo0, p + 1)
                    for m in range(C):
                        last = split_product(pe, keyq[:, m, :], lambda w, c: w[:, c, P * m:P * (m + 1)], w_kq,
                                             lambda h, c: h[:, s, c, :], (h_hi0, h_lo0))
                    last.then_inc(s_keyq, 1)
                if live(4):
                    p, s = pair(t, at - 4)
                    pe.wait_ge(s_w3, p + 1)
                    last = pe.transpose(w3row, w3[:, s], ident[:, :])
                    last.then_inc(s_w3row, 1)
                if live(2):
                    p, s = pair(t, at - 2)
                    pe.wait_ge(s_norm2, p + 1)
                    for j in range(G):
                        for c in range(C):
                            last = pe.transpose(turn2[:, c, N * j:N * (j + 1)], normed2[:, s, j, P * c:P * (c + 1)],
                                                ident[:, :])
                    last.then_inc(s_turn2, 1)
                if live(0):
                    p, s = pair(t, at - 0)
                    if first(p):
                        pe.wait_ge(s_lower0, 2)
                    for j in range(G):
                        last = split_product(pe, val0[:, j, 0:D + 2], lambda h, c: h[:, s, c, N * j:N * (j + 1)], (h_hi0, h_lo0),
                                             lambda w, c: w[:, c, :], w_v0)
                    last.then_inc(s_val0, 1)
                if live(0):
                    p, s = pair(t, at - 0)
                    pe.wait_ge(s_keyq_out, p + 1)
                    for j in range(G):
                        for c in range(C):
                            last = pe.matmul(score0[:, N * j:N * (j + 1)], keyq_sb[:, s, c, N * j:N * (j + 1)],
                                             h0[:, s, c, N * j:N * (j + 1)], start=(c == 0), stop=(c == C - 1))
                    last.then_inc(s_score0, 1)
                if live(2):
                    p, s = pair(t, at - 2)
                    if first(p):
                        pe.wait_ge(s_lower2, 1)
                    pe.wait_ge(s_lo2, p + 1)
                    if exists(p - 2):
                        pe.wait_ge(s_exp3, p - 1)
                    for j in range(G):
                        last = split_product(pe, wh[:, j, 0:D + 2], lambda h, c: h[:, s, c, N * j:N * (j + 1)], (h_hi2, h_lo2),
                                             lambda w, c: w[:, c, :], w_wh)
                if live(4):
                    p, s = pair(t, at - 4)
                    count = held(pe, p + 1)
                    pe.wait_ge(s_constants, 3)
                    pe.wait_ge(s_soft3, count)
                    last = pe.transpose(w3col, soft3[:, s], ident[0:G, 0:G])
                    last.then_inc(s_w3col, 1)
                if live(1):
                    p, s = pair(t, at - 1)
                    pe.wait_ge(s_trans, p + 1)
                    for j in range(G):
                        last = pe.transpose(transT[:, N * j:N * (j + 1)], trans[:, s, j], ident[:, :])
                    last.then_inc(s_transT, 1)
                if live(3):
                    p, s = pair(t, at - 3)
                    pe.wait_ge(s_norm3, p + 1)
                    for j in range(G):
                        for c in range(C):
                            last = pe.transpose(turn3[:, c, N * j:N * (j + 1)], normed3[:, s, j, P * c:P * (c + 1)],
                                                ident[:, :])
                    last.then_inc(s_turn3, 1)

            run(pe, step)

        @block.vector
        def _(vec):
            vec.memset(ones_r[:, :].bitcast(F32), 1.0).then_inc(s_constants_v, 1)
            vec.memset(hop_bias[64:P, :].bitcast(F32), 0.0).then_inc(s_constants_v, 1)
            for s in range(2):
                vec.memset(val0_sb[:, s, :, D + 1], 1.0).then_inc(s_constants_v, 1)
            vec.wait_ge(s_load_bias, 16)
            for j in range(G):
                vec.tensor_scalar(value_bias[:, j, :], value_row[:, :], -1.0, None, ALU.add).then_inc(s_constants_v, 1)

            def attention_columns(start, to):
                vec.tensor_copy(w_all[:, :, to:to + 2], vectors[:, start:start + 2 * C]
                                .rearrange("p (m v) -> p m v", m=C)).then_inc(s_vectors, 1)

            def split_lower0():
                vec.wait_ge(s_products, 1)
                vec.tensor_copy(vectors[:, :], small[:, 0:13]).then_inc(s_vectors, 1)
                vec.wait_ge(s_upper0, 2)
                vec.tensor_tensor(w_lo[:, :, KQ:KB + 1], keyq_weights, w_hi[:, :, KQ:KB + 1].bitcast(F32),
                                  ALU.subtract).then_inc(s_lower0, 1)
                vec.tensor_tensor(w_lo[:, :, V0:HOP2], w_all[:, :, V0:HOP2], w_hi[:, :, V0:HOP2].bitcast(F32),
                                  ALU.subtract).then_inc(s_lower0, 1)

            def split_lower1():
                vec.wait_ge(s_vectors, 1)
                vec.wait_ge(s_load_w1, 16)
                attention_columns(5, HOP2 + D)
                vec.wait_ge(s_load_hops, 16 * 3)
                for j in range(G):
                    vec.tensor_scalar(sij_const[:, j, 0:1], vectors[:, 3:4], ab_col[:, 0:1], None,
                                      ALU.add).then_inc(s_vectors, 1)
                    vec.tensor_copy(sij_const[:, j, 1:2], vectors[:, 4:5]).then_inc(s_vectors, 1)
                vec.tensor_copy(hop_bias[0:32, :], hop_rows[0:32, :]).then_inc(s_lower1, 1)
                vec.tensor_copy(hop_rows_hi[32:64, :], hop_rows[32:64, :]).then_inc(s_lower1, 1)
                vec.wait_ge(s_lower1, 2)
                vec.tensor_tensor(hop_bias[32:64, :], hop_rows[32:64, :], hop_rows_hi[32:64, :].bitcast(F32),
                                  ALU.subtract).then_inc(s_lower1, 1)
                vec.wait_ge(s_upper1, 1)
                vec.tensor_tensor(w_lo[:, :, HOP2:WH], w_all[:, :, HOP2:WH], w_hi[:, :, HOP2:WH].bitcast(F32),
                                  ALU.subtract).then_inc(s_lower1, 1)

            def split_lower2():
                vec.wait_ge(s_vectors, 6)
                vec.wait_ge(s_load_w2, 16)
                attention_columns(9, WH + D)
                vec.wait_ge(s_upper2, 1)
                vec.tensor_tensor(w_lo[:, :, WH:W_COLS], w_all[:, :, WH:W_COLS],
                                  w_hi[:, :, WH:W_COLS].bitcast(F32), ALU.subtract).then_inc(s_lower2, 1)

            def step(t, at, live):
                if live(1):
                    p, s = pair(t, at - 1)
                    vec.wait_ge(s_aggr1, p + 1)
                    vec.tensor_scalar(negmean1[:, s], moments1[:, s, :, 0], -1.0, None, ALU.mult)
                    last = vec.tensor_scalar(vareps1[:, s], moments1[:, s, :, 1], LN_EPS, None, ALU.add)
                    last.then_inc(s_mom1, 1)
                if live(0):
                    p, s = pair(t, at - 0)
                    vec.wait_ge(s_load_x[s], loads(t, at - 0))
                    for j in range(G):
                        last = vec.bn_stats(stats0[:, s, j], x0[:, s, j])
                    last.then_inc(s_stat0, 1)
                if live(0):
                    p, s = pair(t, at - 0)
                    vec.wait_ge(s_stat0, p + 1)
                if live(3):
                    p, s = pair(t, at - 3)
                    vec.wait_ge(s_penalty, p + 1)
                    vec.wait_ge(s_wh1row, p + 1)
                    for j in range(G):
                        last = vec.scalar_tensor_tensor(z2[:, s, j], wh1row[:, N * j:N * (j + 1)], wh_sb[:, s, j, D + 1:D + 2],
                                                        penalty[:, s, j], ALU.add, ALU.add)
                    last.then_inc(s_z2, 1)
                if live(0):
                    p, s = pair(t, at - 0)
                    for j in range(G):
                        last = vec.bn_aggr(moments0[:, s, j], stats0[:, s, j])
                    last.then_inc(s_aggr0, 1)
                if live(3):
                    p, s = pair(t, at - 3)
                    vec.wait_ge(s_z2, p + 1)
                    last = vec.scalar_tensor_tensor(leaky2[:, s], z2[:, s], SLOPE, z2[:, s], ALU.mult, ALU.max)
                    last.then_inc(s_leaky2, 1)
                if live(0):
                    p, s = pair(t, at - 0)
                    vec.wait_ge(s_aggr0, p + 1)
                    vec.tensor_scalar(negmean0[:, s], moments0[:, s, :, 0], -1.0, None, ALU.mult)
                    last = vec.tensor_scalar(vareps0[:, s], moments0[:, s, :, 1], LN_EPS, None, ALU.add)
                    last.then_inc(s_mom0, 1)
                if live(3):
                    p, s = pair(t, at - 3)
                    vec.wait_ge(s_leaky2, p + 1)
                    last = vec.tensor_reduce(max2[:, s], leaky2[:, s], AX.X, ALU.max)
                    last.then_inc(s_max2, 1)
                if live(3):
                    p, s = pair(t, at - 3)
                    vec.wait_ge(s_max2, p + 1)
                    last = vec.tensor_scalar(negmax2[:, s], max2[:, s], -1.0, None, ALU.mult)
                    last.then_inc(s_negmax2, 1)
                if live(3):
                    p, s = pair(t, at - 3)
                    vec.wait_ge(s_exp2, p + 1)
                    last = vec.reciprocal(suminv2[:, s], sum2[:, s])
                    last.then_inc(s_suminv2, 1)
                if live(3):
                    p, s = pair(t, at - 3)
                    vec.wait_ge(s_suminv2, p + 1)
                    last = vec.tensor_tensor(att2[:, s], exp2[:, s], suminv2[:, s].unsqueeze(2).broadcast_to([P, G, N]), ALU.mult)
                    last.then_inc(s_att2, 1)
                if live(1):
                    p, s = pair(t, at - 1)
                    vec.wait_ge(s_hi1, p + 1)
                    vec.wait_ge(s_turn1, p + 1)
                    last = vec.scalar_tensor_tensor(h_lo1[:, s], turn1, 0.0, h_hi1[:, s].bitcast(F32), ALU.max, ALU.subtract)
                    last.then_inc(s_lo1, 1)
                if live(2):
                    p, s = pair(t, at - 2)
                    vec.wait_ge(s_hop0_0, p + 1)
                    last = vec.scalar_tensor_tensor(x2[:, s], hop0, 0.0, x1[:, s], ALU.max, ALU.add)
                    last.then_inc(s_x2, 1)
                if live(0):
                    p, s = pair(t, at - 0)
                    if first(p):
                        split_lower0()
                    vec.wait_ge(s_h0, p + 1)
                    last = vec.tensor_copy(h_hi0[:, s], h0[:, s])
                    last.then_inc(s_hi0, 1)
                if live(2):
                    p, s = pair(t, at - 2)
                    vec.wait_ge(s_x2, p + 1)
                    for j in range(G):
                        last = vec.bn_stats(stats2[:, s, j], x2[:, s, j])
                    last.then_inc(s_stat2, 1)
                if live(2):
                    p, s = pair(t, at - 2)
                    count = held(vec, p + 1)
                    vec.wait_ge(s_constants_v, CONSTANTS_V)
                    vec.wait_ge(s_stat2, count)
                    for j in range(G):
                        last = vec.bn_aggr(moments2[:, s, j], stats2[:, s, j])
                    last.then_inc(s_aggr2, 1)
                if live(2):
                    p, s = pair(t, at - 2)
                    vec.wait_ge(s_aggr2, p + 1)
                    vec.tensor_scalar(negmean2[:, s], moments2[:, s, :, 0], -1.0, None, ALU.mult)
                    last = vec.tensor_scalar(vareps2[:, s], moments2[:, s, :, 1], LN_EPS, None, ALU.add)
                    last.then_inc(s_mom2, 1)
                if live(1):
                    p, s = pair(t, at - 1)
                    if first(p):
                        split_lower2()
                    vec.wait_ge(s_hop2_out, p + 1)
                    last = vec.tensor_tensor(sij[:, s], hop2_sb[:, s, :, D:D + 2], sij_const[:, :, :], ALU.add)
                    last.then_inc(s_sij, 1)
                if live(4):
                    p, s = pair(t, at - 4)
                    vec.wait_ge(s_adjk, p + 1)
                    for j in range(G):
                        last = vec.scalar_tensor_tensor(w3_prod[:, s, j], adjk[:, j, :], INV_SCALE, vqk_sb[:, s, j, D:D + ATT],
                                                        ALU.mult, ALU.mult, accum_out=w3[:, s, j:j + 1])
                    last.then_inc(s_w3, 1)
                if live(3):
                    p, s = pair(t, at - 3)
                    vec.wait_ge(s_elu_exp, p + 1)
                    vec.wait_ge(s_mix2, p + 1)
                    last = vec.scalar_tensor_tensor(elu_pos[:, s], mix2, 0.0, x2[:, s], ALU.max, ALU.add)
                    last.then_inc(s_elu_pos, 1)
                if live(3):
                    p, s = pair(t, at - 3)
                    vec.wait_ge(s_elu_pos, p + 1)
                    last = vec.scalar_tensor_tensor(x3[:, s], elu_exp[:, s], 1.0, elu_pos[:, s], ALU.min, ALU.add)
                    last.then_inc(s_x3, 1)
                if live(1):
                    p, s = pair(t, at - 1)
                    vec.wait_ge(s_z1, p + 1)
                    last = vec.scalar_tensor_tensor(leaky1[:, s], z1[:, s], SLOPE, z1[:, s], ALU.mult, ALU.max)
                    last.then_inc(s_leaky1, 1)
                if live(3):
                    p, s = pair(t, at - 3)
                    vec.wait_ge(s_x3, p + 1)
                    for j in range(G):
                        last = vec.bn_stats(stats3[:, s, j], x3[:, s, j])
                    last.then_inc(s_stat3, 1)
                if live(4):
                    p, s = pair(t, at - 4)
                    vec.wait_ge(s_w3row, p + 1)
                    last = vec.tensor_reduce(max3[:, s], w3row, AX.X, ALU.max)
                    last.then_inc(s_max3, 1)
                if live(3):
                    p, s = pair(t, at - 3)
                    count = held(vec, p + 1)
                    vec.wait_ge(s_constants_v, CONSTANTS_V)
                    vec.wait_ge(s_stat3, count)
                    for j in range(G):
                        last = vec.bn_aggr(moments3[:, s, j], stats3[:, s, j])
                    last.then_inc(s_aggr3, 1)
                if live(4):
                    p, s = pair(t, at - 4)
                    vec.wait_ge(s_max3, p + 1)
                    last = vec.tensor_scalar(negmax3[:, s], max3[:, s], -1.0, None, ALU.mult)
                    last.then_inc(s_negmax3, 1)
                if live(3):
                    p, s = pair(t, at - 3)
                    vec.wait_ge(s_aggr3, p + 1)
                    vec.tensor_scalar(negmean3[:, s], moments3[:, s, :, 0], -1.0, None, ALU.mult)
                    last = vec.tensor_scalar(vareps3[:, s], moments3[:, s, :, 1], LN_EPS, None, ALU.add)
                    last.then_inc(s_mom3, 1)
                if live(2):
                    p, s = pair(t, at - 2)
                    vec.wait_ge(s_hi2, p + 1)
                    vec.wait_ge(s_turn2, p + 1)
                    last = vec.scalar_tensor_tensor(h_lo2[:, s], turn2, 0.0, h_hi2[:, s].bitcast(F32), ALU.max, ALU.subtract)
                    last.then_inc(s_lo2, 1)
                if live(1):
                    p, s = pair(t, at - 1)
                    vec.wait_ge(s_exp1, p + 1)
                    vec.wait_ge(s_load_adj1[s], loads(t, at - 1))
                    for j in range(G):
                        last = vec.scalar_tensor_tensor(alpha[:, s, j], exp1[:, s, j], 1.0, adj1[:, s, j], ALU.mult, ALU.mult,
                                                        accum_out=rowsum1[:, s, j:j + 1])
                    last.then_inc(s_alpha, 1)
                if live(0):
                    p, s = pair(t, at - 0)
                    if first(p):
                        split_lower1()
                    vec.wait_ge(s_val0_out, p + 1)
                    last = vec.tensor_scalar(kbias[:, s], val0_sb[:, s, :, 0], vectors[:, 2:3], None, ALU.add)
                    last.then_inc(s_kbias, 1)
                if live(4):
                    p, s = pair(t, at - 4)
                    vec.wait_ge(s_exp3, p + 1)
                    last = vec.reciprocal(suminv3[:, s], sum3[:, s])
                    last.then_inc(s_suminv3, 1)
                if live(1):
                    p, s = pair(t, at - 1)
                    vec.wait_ge(s_alpha, p + 1)
                    last = vec.tensor_scalar(rowsum1e[:, s], rowsum1[:, s], ROWSUM_EPS, None, ALU.add)
                    last.then_inc(s_rowsum1e, 1)
                if live(1):
                    p, s = pair(t, at - 1)
                    vec.wait_ge(s_rowsum1e, p + 1)
                    last = vec.reciprocal(rowinv1[:, s], rowsum1e[:, s])
                    last.then_inc(s_rowinv1, 1)
                if live(4):
                    p, s = pair(t, at - 4)
                    vec.wait_ge(s_suminv3, p + 1)
                    last = vec.tensor_scalar(soft3[:, s], exp3[:, s], suminv3[:, s], None, ALU.mult)
                    last.then_inc(s_soft3, 1)
                if live(1):
                    p, s = pair(t, at - 1)
                    vec.wait_ge(s_rowinv1, p + 1)
                    last = vec.tensor_tensor(trans[:, s], alpha[:, s], rowinv1[:, s].unsqueeze(2).broadcast_to([P, G, N]), ALU.mult)
                    last.then_inc(s_trans, 1)
                if live(0):
                    p, s = pair(t, at - 0)
                    vec.wait_ge(s_exp0, p + 1)
                    vec.wait_ge(s_load_adjT0[s], loads(t, at - 0))
                    last = vec.tensor_tensor(att0[:, s], exp0[:, s], adjT0[:, s], ALU.mult)
                    last.then_inc(s_att0, 1)
                if live(2):
                    p, s = pair(t, at - 2)
                    vec.wait_ge(s_load_adjT2[s], loads(t, at - 2))
                    last = vec.tensor_scalar(penalty[:, s], adjT2[:, s], 0.5, MASKED_Z, ALU.is_le, ALU.mult)
                    last.then_inc(s_penalty, 1)
                if live(4):
                    p, s = pair(t, at - 4)
                    vec.wait_ge(s_w3col_out, p + 1)
                    if exists(p - 2):
                        vec.wait_ge(s_store[s], loads(t, at - 4 - 2))
                    for j in range(G):
                        last = vec.scalar_tensor_tensor(y[:, s, j], vqk_sb[:, s, j, 0:D], w3col_sb[:, s, j:j + 1], x3[:, s, j],
                                                        ALU.mult, ALU.add)
                    last.then_inc(s_out, 1)
                if live(0):
                    p, s = pair(t, at - 0)
                    vec.wait_ge(s_mix0, p + 1)
                    last = vec.reciprocal(rowinv0[:, s], mix0[:, :, D])
                    last.then_inc(s_rowinv0, 1)
                if live(3):
                    p, s = pair(t, at - 3)
                    vec.wait_ge(s_hi3, p + 1)
                    last = vec.scalar_tensor_tensor(h_lo3[:, s], turn3, 0.0, h_hi3[:, s].bitcast(F32), ALU.max, ALU.subtract)
                    last.then_inc(s_lo3, 1)
                if live(0):
                    p, s = pair(t, at - 0)
                    vec.wait_ge(s_rowinv0, p + 1)
                    vec.wait_ge(s_xb, p + 1)
                    for j in range(G):
                        last = vec.scalar_tensor_tensor(x1[:, s, j], mix0[:, j, 0:D], rowinv0[:, s, j:j + 1], xb[:, s, j],
                                                        ALU.mult, ALU.add)
                    last.then_inc(s_x1, 1)
                if live(0):
                    p, s = pair(t, at - 0)
                    vec.wait_ge(s_x1, p + 1)
                    for j in range(G):
                        last = vec.bn_stats(stats1[:, s, j], x1[:, s, j])
                    last.then_inc(s_stat1, 1)
                if live(0):
                    p, s = pair(t, at - 0)
                    count = held(vec, p + 1)
                    vec.wait_ge(s_constants_v, CONSTANTS_V)
                    vec.wait_ge(s_stat1, count)
                    for j in range(G):
                        last = vec.bn_aggr(moments1[:, s, j], stats1[:, s, j])
                    last.then_inc(s_aggr1, 1)

            run(vec, step)


def kernel(**inputs):
    import numpy as np
    import concourse.bacc as bacc
    from concourse.bass_utils import run_bass_kernel_spmd

    a = {name: np.asarray(value) for name, value in inputs.items()}
    graphs, nodes, features = a["x"].shape

    def by_pair(v):
        return np.ascontiguousarray(v.reshape(graphs // G, G, nodes, -1).transpose(0, 2, 1, 3))

    def by_half(v):
        return np.ascontiguousarray(v.reshape(features // P, P, -1).transpose(1, 0, 2))

    zeros = np.zeros((features, 2), np.float32)
    weights = np.concatenate([
        a["L0_gnn_Wv_w"].T, zeros[:, 0:1], a["L1_gnn_Wk"][2], zeros, a["L1_gnn_Wk"][1], a["L1_gnn_Wk"][0],
        a["L2_gnn_W"], zeros, a["L3_gnn_W_v"].T, a["L3_gnn_W_qk"].T], 1)
    aw, ag = a["L1_gnn_aw"].reshape(2, features), a["L2_gnn_a"].reshape(2, features)
    setup = np.concatenate([
        a["L0_gnn_Wk_w"], a["L0_gnn_Wq_w"], a["L0_gnn_Wq_b"][:, None], a["L0_gnn_Wk_b"][:, None],
        a["L1_gnn_Wv"].T, aw[::-1].T, a["L1_gnn_bv"][:, None], a["L2_gnn_W"].T, ag.T], 1)
    arrays = {
        "x_in": by_pair(a["x"]), "adj_in": by_pair(a["adj"]), "adjT_in": by_pair(a["adj"].transpose(0, 2, 1)),
        "weights_in": by_half(weights), "setup_in": by_half(setup), "hop_bias_in": a["L1_gnn_bk"],
        "value_bias_in": a["L0_gnn_Wv_b"], "ab_in": a["L1_gnn_ab"]}
    nc = bacc.Bacc("TRN2", target_bir_lowering=False, num_devices=1)
    args = [nc.dram_tensor(name, v.shape, F32, kind="ExternalInput").ap() for name, v in arrays.items()]
    y = nc.dram_tensor("y_out", arrays["x_in"].shape, F32, kind="ExternalOutput").ap()
    graph_layers_kernel(nc, *args, y)
    result = run_bass_kernel_spmd(nc, [arrays], core_ids=[0]).results[0]["y_out"]
    return np.asarray(result).transpose(0, 2, 1, 3).reshape(graphs, nodes, features)
```

```python
from contextlib import ExitStack

import concourse.bass as bass
from concourse import mybir

ALU = mybir.AluOpType
ACT = mybir.ActivationFunctionType
AX = mybir.AxisListType
F32 = mybir.dt.float32
F32R = mybir.dt.float32r

P = 128
LN_EPS = 1e-5
ROWSUM_EPS = 1e-12
SLOPE = 0.2
MASKED = -9e15
MASKED_Z = MASKED / SLOPE
G = 2
PAIRS = 32
STAGES = 7

D_ = 256
KQ, KB, V0 = 0, 256, 257
HOP2, HOP1, HOP0 = 514, 772, 1028
WH, VQK, W_COLS = 1284, 1542, 1926
S_WK, S_WQ, S_BQ, S_BK, S_WV1, S_A1, S_BV1, S_WG, S_AG = 0, 256, 512, 513, 514, 770, 772, 773, 1029
S_COLS = 1031


def pair(t, at):
    return 2 * t + at, at % 2


def exists(p):
    return not isinstance(p, int) or p >= 0


def first(p):
    return isinstance(p, int) and p == 0


def upto(count):
    return min(count, PAIRS) if isinstance(count, int) else count


def held(eng, count):
    return count if isinstance(count, int) else eng.snap(count)


def loads(t, at):
    return 16 * (t + at // 2) + 16


def accumulate(pe, out, terms, start=False, stop=False):
    steps = [(a[:, c], b[:, c]) for c in range(2) for a, b in terms]
    for n, (a, b) in enumerate(steps):
        last = pe.matmul(out, a, b, start=(start and n == 0), stop=(stop and n == len(steps) - 1))
    return last


def graph_layers_kernel(nc: bass.Bass, x_in, adj_in, adjT_in, weights_in, setup_in, hop_bias_in, value_bias_in,
                        ab_in, y_out):
    pairs, N, _, D = x_in.shape
    assert pairs == PAIRS and N == P and D == D_
    C = D // P
    ATT = 64
    QK = 2 * ATT
    INV_SCALE = ATT ** -0.5

    with ExitStack() as ctx:
        def sb(name, *shape, dt=F32):
            return ctx.enter_context(nc.sbuf_tensor(name, [P, *shape], dt))

        def sem(name):
            return ctx.enter_context(nc.semaphore(name))

        ident = sb("ident", P)
        minus_half = sb("minus_half", G)
        ones_r = sb("ones_r", P, dt=F32R)
        w_all = sb("w_all", C, W_COLS)
        w_hi = sb("w_hi", C, W_COLS, dt=F32R)
        w_lo = sb("w_lo", C, W_COLS, dt=F32R)
        w_setup = sb("w_setup", C, S_COLS)
        hop_rows = sb("hop_rows", D)
        hop_rows_hi = sb("hop_rows_hi", D, dt=F32R)
        hop_bias = sb("hop_bias", D, dt=F32R)
        value_row = sb("value_row", D)
        value_bias = sb("value_bias", G, D)
        ab_col = sb("ab_col", 1)
        vectors = sb("vectors", 13)
        sij_const = sb("sij_const", 1)

        def parts(start, width):
            return w_hi[:, :, start:start + width], w_lo[:, :, start:start + width]

        w_v0, w_hop2, w_wh = parts(KB, D + 2), parts(HOP2, D + 2), parts(WH, D + 2)
        w_hop1, w_hop0, w_vqk, w_kq = parts(HOP1, D), parts(HOP0, D), parts(VQK, D + QK), parts(KQ, D)

        x0, x1, x2, x3, y, xb = (sb(n, 2, G, D) for n in ("x0", "x1", "x2", "x3", "y", "xb"))
        adjT0, adj1, adjT2 = (sb(n, 2, G, N) for n in ("adjT0", "adj1", "adjT2"))
        stats0, stats1, stats2, stats3 = (sb(f"stats{n}", 2, G, 6) for n in range(4))
        moments0, moments1, moments2, moments3 = (sb(f"moments{n}", 2, G, 2) for n in range(4))
        negmean0, negmean1, negmean2, negmean3 = (sb(f"negmean{n}", 2, G) for n in range(4))
        vareps0, vareps1, vareps2, vareps3 = (sb(f"vareps{n}", 2, G) for n in range(4))
        rstd0, rstd1, rstd2, rstd3 = (sb(f"rstd{n}", 2, G) for n in range(4))
        normed0, normed1, normed2, normed3 = (sb(f"normed{n}", 2, G, D) for n in range(4))
        h0 = sb("h0", 2, C, G * N)
        h_hi0, h_hi1, h_hi2, h_hi3 = (sb(f"h_hi{n}", 2, C, G * N, dt=F32R) for n in range(4))
        h_lo0, h_lo1, h_lo2, h_lo3 = (sb(f"h_lo{n}", 2, C, G * N, dt=F32R) for n in range(4))
        keyq_sb = sb("keyq_sb", 2, C, G * N)
        val0_sb = sb("val0_sb", 2, G, D + 2)
        kbias, rowinv0 = sb("kbias", 2, G), sb("rowinv0", 2, G)
        exp0, att0 = sb("exp0", 2, G, N), sb("att0", 2, G, N)
        hop2_upper, hop1_upper = sb("hop2_upper", 2, G, D, dt=F32R), sb("hop1_upper", 2, G, D, dt=F32R)
        hop2_rest, hop1_rest = sb("hop2_rest", 2, G, D, dt=F32R), sb("hop1_rest", 2, G, D, dt=F32R)
        hop2_cols = sb("hop2_cols", 2, G, 2)
        si = sb("si", 2, G)
        z1, leaky1, exp1, alpha, trans = (sb(n, 2, G, N) for n in ("z1", "leaky1", "exp1", "alpha", "trans"))
        rowsum1, rowsum1e, rowinv1 = (sb(n, 2, G) for n in ("rowsum1", "rowsum1e", "rowinv1"))
        transT_upper, transT_rest = (sb(n, 2, G * N, dt=F32R) for n in ("transT_upper", "transT_rest"))
        wh_sb = sb("wh_sb", 2, G, D + 2)
        penalty, z2, leaky2, exp2, att2 = (sb(n, 2, G, N) for n in ("penalty", "z2", "leaky2", "exp2", "att2"))
        negmax2, sum2, suminv2 = (sb(n, 2, G) for n in ("negmax2", "sum2", "suminv2"))
        w_place = w_all[:, :, :].rearrange("p c w -> p (c w)")
        elu_exp, elu_pos = (w_place[:, n * 2 * G * D:(n + 1) * 2 * G * D]
                            .rearrange("p (s j d) -> p s j d", s=2, j=G) for n in range(2))
        vqk_sb = (w_place[:, 4 * G * D:4 * G * D + 2 * G * (D + QK)]
                  .rearrange("p (s j d) -> p s j d", s=2, j=G))
        w3_prod, w3, w3col_sb = sb("w3_prod", 2, G, ATT), sb("w3", 2, G), sb("w3col_sb", 2, G)

        def rows(name, width):
            return ctx.enter_context(nc.sbuf_tensor(name, [G, 2, width], F32))

        negmax3, sum3, suminv3 = (rows(n, 1) for n in ("negmax3", "sum3", "suminv3"))
        exp3, soft3 = rows("exp3", N), rows("soft3", N)

        psum = ctx.enter_context(nc.psum_tensor("psum", [P, 8, 512], F32))
        turn0 = psum[:, 1].rearrange("p (c n) -> p c n", c=C)
        keyq = psum[:, 6].rearrange("p (c n) -> p c n", c=C)
        val0 = psum[:, 4:6]
        score0 = psum[:, 6, 0:G * N]
        mix0 = psum[:, 6:8]
        turn1 = psum[:, 7].rearrange("p (c n) -> p c n", c=C)
        hop2 = psum[:, 4:6]
        sjrow = psum[:, 2, 0:G * N]
        transT = psum[:, 7, 0:G * N]
        hop1 = psum[:, 0].rearrange("p (j d) -> p j d", j=G)
        hop0 = psum[:, 3].rearrange("p (j d) -> p j d", j=G)
        turn2 = psum[:, 5].rearrange("p (c n) -> p c n", c=C)
        wh = psum[:, 1:3]
        wh1row = psum[:, 1, 0:G * N]
        mix2 = psum[:, 2].rearrange("p (j d) -> p j d", j=G)
        turn3 = psum[:, 2].rearrange("p (c n) -> p c n", c=C)
        vqk = psum[:, 0:2]
        adjk = psum[:, 7, 0:G * ATT].rearrange("p (j d) -> p j d", j=G)
        w3row = psum[0:G, 4, 0:N]
        w3col = psum[:, 7, 0:G]

        s_constants = sem("constants")
        s_constants_v = sem("constants_v")
        s_load_bias = sem("load_bias")
        s_load_w0 = sem("load_w0")
        s_load_setup0 = sem("load_setup0")
        s_load_setup1 = sem("load_setup1")
        s_load_hops = sem("load_hops")
        s_load_w1 = sem("load_w1")
        s_load_w2 = sem("load_w2")
        s_products = sem("products")
        s_vectors = sem("vectors")
        s_upper0 = sem("upper0")
        s_upper1 = sem("upper1")
        s_upper2 = sem("upper2")
        s_lower0 = sem("lower0")
        s_lower1 = sem("lower1")
        s_lower2 = sem("lower2")
        s_load_x = [sem(f"load_x_{i}") for i in range(2)]
        s_load_adjT0 = [sem(f"load_adjT0_{i}") for i in range(2)]
        s_stat0 = sem("stat0")
        s_aggr0 = sem("aggr0")
        s_mom0 = sem("mom0")
        s_rstd0 = sem("rstd0")
        s_norm0_0 = sem("norm0_0")
        s_norm0_1 = sem("norm0_1")
        s_turn0_0 = sem("turn0_0")
        s_hi0 = sem("hi0")
        s_lo0 = sem("lo0")
        s_h0 = sem("h0")
        s_xb = sem("xb")
        s_keyq_lo = sem("keyq_lo")
        s_keyq_out = sem("keyq_out")
        s_val0_lo = sem("val0_lo")
        s_val0_out = sem("val0_out")
        s_kbias = sem("kbias")
        s_score0 = sem("score0")
        s_exp0 = sem("exp0")
        s_att0 = sem("att0")
        s_mix0 = sem("mix0")
        s_rowinv0 = sem("rowinv0")
        s_x1 = sem("x1")
        s_load_adj1 = [sem(f"load_adj1_{i}") for i in range(2)]
        s_stat1 = sem("stat1")
        s_aggr1 = sem("aggr1")
        s_mom1 = sem("mom1")
        s_rstd1 = sem("rstd1")
        s_norm1_0 = sem("norm1_0")
        s_norm1_1 = sem("norm1_1")
        s_turn1_1 = sem("turn1_1")
        s_hi1 = sem("hi1")
        s_lo1 = sem("lo1")
        s_hop2_lo = sem("hop2_lo")
        s_hop2_up = sem("hop2_up")
        s_hop2_cols = sem("hop2_cols")
        s_hop2_rest = sem("hop2_rest")
        s_si = sem("si")
        s_sjrow = sem("sjrow")
        s_z1 = sem("z1")
        s_leaky1 = sem("leaky1")
        s_exp1 = sem("exp1")
        s_alpha = sem("alpha")
        s_rowsum1e = sem("rowsum1e")
        s_rowinv1 = sem("rowinv1")
        s_trans = sem("trans")
        s_transT = sem("transT")
        s_transT_up = sem("transT_up")
        s_transT_rest = sem("transT_rest")
        s_hop1_t = sem("hop1_t")
        s_hop1_up = sem("hop1_up")
        s_hop1_rest = sem("hop1_rest")
        s_hop0_t = sem("hop0_t")
        s_x2 = sem("x2")
        s_load_adjT2 = [sem(f"load_adjT2_{i}") for i in range(2)]
        s_stat2 = sem("stat2")
        s_aggr2 = sem("aggr2")
        s_mom2 = sem("mom2")
        s_rstd2 = sem("rstd2")
        s_norm2_0 = sem("norm2_0")
        s_norm2_1 = sem("norm2_1")
        s_turn2_1 = sem("turn2_1")
        s_hi2 = sem("hi2")
        s_lo2 = sem("lo2")
        s_penalty = sem("penalty")
        s_wh_lo = sem("wh_lo")
        s_wh_out = sem("wh_out")
        s_wh1row = sem("wh1row")
        s_z2 = sem("z2")
        s_leaky2 = sem("leaky2")
        s_max2 = sem("max2")
        s_exp2 = sem("exp2")
        s_suminv2 = sem("suminv2")
        s_att2 = sem("att2")
        s_mix2 = sem("mix2")
        s_elu_exp = sem("elu_exp")
        s_elu_pos = sem("elu_pos")
        s_x3 = sem("x3")
        s_stat3 = sem("stat3")
        s_aggr3 = sem("aggr3")
        s_mom3 = sem("mom3")
        s_rstd3 = sem("rstd3")
        s_norm3_0 = sem("norm3_0")
        s_norm3_1 = sem("norm3_1")
        s_turn3_0 = sem("turn3_0")
        s_hi3 = sem("hi3")
        s_lo3 = sem("lo3")
        s_vqk_lo = sem("vqk_lo")
        s_vqk_out = sem("vqk_out")
        s_adjk = sem("adjk")
        s_w3 = sem("w3")
        s_w3row = sem("w3row")
        s_max3 = sem("max3")
        s_exp3 = sem("exp3")
        s_suminv3 = sem("suminv3")
        s_soft3 = sem("soft3")
        s_w3col = sem("w3col")
        s_w3col_out = sem("w3col_out")
        s_out = sem("out")
        s_store = [sem(f"store_{i}") for i in range(2)]

        CONSTANTS_V = 6
        keyq_weights = psum[:, 2:2 + C, 0:D + 1]
        small = psum[:, 0]
        block = ctx.enter_context(nc.Block())

        def run(eng, step):
            full_from = (STAGES + 3) // 2
            for k in range(2 * full_from):
                step(0, k, lambda g: 0 <= k - g < PAIRS)
            with eng.Fori(full_from, PAIRS // 2) as t:
                for c in range(2):
                    step(t, c, lambda g: True)
            for k in range(PAIRS, PAIRS + STAGES):
                step(0, k, lambda g: 0 <= k - g < PAIRS)

        @block.sync
        def _(sync):
            sync.dma_start(w_setup[:, :, 0:S_WV1], setup_in[:, :, 0:S_WV1]).then_inc(s_load_setup0, 16)

            def load_w(start, end, loaded):
                sync.dma_start(w_all[:, :, start:end], weights_in[:, :, start - V0:end - V0]).then_inc(loaded, 16)

            def load_weights0():
                sync.dma_start(w_setup[:, :, S_WV1:S_COLS], setup_in[:, :, S_WV1:S_COLS]).then_inc(s_load_setup1, 16)
                load_w(V0, HOP2, s_load_w0)
                sync.dma_start(value_row[:, :], value_bias_in.partition_broadcast(P)).then_inc(s_load_bias, 16)

            def load_weights1():
                load_w(HOP2, WH, s_load_w1)
                sync.dma_start(ab_col[:, :], ab_in.partition_broadcast(P)).then_inc(s_load_hops, 16)
                sync.wait_ge(s_constants, 1)
                for q in (0, 32):
                    sync.dma_start(hop_rows[q:q + 3, :], hop_bias_in).then_inc(s_load_hops, 16)

            def load_weights2():
                load_w(WH, W_COLS, s_load_w2)

            def step(t, at, live):
                if live(0):
                    p, s = pair(t, at - 0)
                    if exists(p - 2):
                        sync.wait_ge(s_xb, p - 1)
                    last = sync.dma_start(x0[:, s], x_in[p])
                    last.then_inc(s_load_x[s], 16)
                if live(4):
                    p, s = pair(t, at - 4)
                    if exists(p - 2):
                        sync.wait_ge(s_adjk, p - 1)
                    last = sync.dma_start(adjT2[:, s], adjT_in[p])
                    last.then_inc(s_load_adjT2[s], 16)
                if live(0):
                    p, s = pair(t, at - 0)
                    if first(p):
                        load_weights0()
                        load_weights1()
                        load_weights2()
                    if exists(p - 2):
                        sync.wait_ge(s_att0, p - 1)
                    last = sync.dma_start(adjT0[:, s], adjT_in[p])
                    last.then_inc(s_load_adjT0[s], 16)
                if live(2):
                    p, s = pair(t, at - 2)
                    last = sync.dma_start(adj1[:, s], adj_in[p])
                    last.then_inc(s_load_adj1[s], 16)
                if live(6):
                    p, s = pair(t, at - 6)
                    sync.wait_ge(s_out, p + 1)
                    last = sync.dma_start(y_out[p], y[:, s])
                    last.then_inc(s_store[s], 16)

            run(sync, step)
            for i in range(2):
                sync.wait_ge(s_store[i], 16 * (PAIRS // 2))

        @block.gpsimd
        def _(pool):
            pool.memset(hop_rows[:, :], 0.0).then_inc(s_constants, 1)
            pool.memset(ident[:, :], 0.0).then_inc(s_constants, 1)
            pool.wait_ge(s_constants, 2)
            pool.affine_select(out=ident[:, :], in_=ident[:, :], compare_op=ALU.not_equal, fill=1.0, base=0,
                               pattern=[[-1, P]], channel_multiplier=1).then_inc(s_constants, 1)
            pool.memset(minus_half[:, :], -0.5).then_inc(s_constants, 1)
            pool.wait_ge(s_constants, 4)

            def step(t, at, live):
                if live(3):
                    p, s = pair(t, at - 3)
                    if first(p):
                        pool.wait_ge(s_constants_v, CONSTANTS_V)
                    last = pool.tensor_tensor(xb[:, s], x0[:, s], value_bias[:, :, :], ALU.add)
                    last.then_inc(s_xb, 1)
                if live(5):
                    p, s = pair(t, at - 5)
                    pool.wait_ge(s_mom2, p + 1)
                    last = pool.tensor_tensor(rstd2[:, s], vareps2[:, s], minus_half[:, :], ALU.pow)
                    last.then_inc(s_rstd2, 1)
                if live(5):
                    p, s = pair(t, at - 5)
                    count = held(pool, p + 1)
                    pool.wait_ge(s_constants, 4)
                    pool.wait_ge(s_rstd2, count)
                    last = pool.tensor_scalar(normed2[:, s, 0], x2[:, s, 0], negmean2[:, s, 0:1], rstd2[:, s, 0:1],
                                              ALU.add, ALU.mult)
                    last.then_inc(s_norm2_0, 1)
                if live(5):
                    p, s = pair(t, at - 5)
                    last = pool.tensor_scalar(normed2[:, s, 1], x2[:, s, 1], negmean2[:, s, 1:2], rstd2[:, s, 1:2],
                                              ALU.add, ALU.mult)
                    last.then_inc(s_norm2_1, 1)
                if live(3):
                    p, s = pair(t, at - 3)
                    pool.wait_ge(s_mom1, p + 1)
                    last = pool.tensor_tensor(rstd1[:, s], vareps1[:, s], minus_half[:, :], ALU.pow)
                    last.then_inc(s_rstd1, 1)
                if live(3):
                    p, s = pair(t, at - 3)
                    count = held(pool, p + 1)
                    pool.wait_ge(s_constants, 4)
                    pool.wait_ge(s_rstd1, count)
                    last = pool.tensor_scalar(normed1[:, s, 0], x1[:, s, 0], negmean1[:, s, 0:1], rstd1[:, s, 0:1],
                                              ALU.add, ALU.mult)
                    last.then_inc(s_norm1_0, 1)
                if live(3):
                    p, s = pair(t, at - 3)
                    last = pool.tensor_scalar(normed1[:, s, 1], x1[:, s, 1], negmean1[:, s, 1:2], rstd1[:, s, 1:2],
                                              ALU.add, ALU.mult)
                    last.then_inc(s_norm1_1, 1)
                if live(6):
                    p, s = pair(t, at - 6)
                    pool.wait_ge(s_mom3, p + 1)
                    last = pool.tensor_tensor(rstd3[:, s], vareps3[:, s], minus_half[:, :], ALU.pow)
                    last.then_inc(s_rstd3, 1)
                if live(6):
                    p, s = pair(t, at - 6)
                    count = held(pool, p + 1)
                    pool.wait_ge(s_constants, 4)
                    pool.wait_ge(s_rstd3, count)
                    last = pool.tensor_scalar(normed3[:, s, 1], x3[:, s, 1], negmean3[:, s, 1:2], rstd3[:, s, 1:2],
                                              ALU.add, ALU.mult)
                    last.then_inc(s_norm3_1, 1)
                if live(6):
                    p, s = pair(t, at - 6)
                    last = pool.tensor_scalar(normed3[:, s, 0], x3[:, s, 0], negmean3[:, s, 0:1], rstd3[:, s, 0:1],
                                              ALU.add, ALU.mult)
                    last.then_inc(s_norm3_0, 1)
                if live(1):
                    p, s = pair(t, at - 1)
                    pool.wait_ge(s_mom0, p + 1)
                    last = pool.tensor_tensor(rstd0[:, s], vareps0[:, s], minus_half[:, :], ALU.pow)
                    last.then_inc(s_rstd0, 1)
                if live(1):
                    p, s = pair(t, at - 1)
                    count = held(pool, p + 1)
                    pool.wait_ge(s_constants, 4)
                    pool.wait_ge(s_rstd0, count)
                    last = pool.tensor_scalar(normed0[:, s, 1], x0[:, s, 1], negmean0[:, s, 1:2], rstd0[:, s, 1:2],
                                              ALU.add, ALU.mult)
                    last.then_inc(s_norm0_1, 1)
                if live(1):
                    p, s = pair(t, at - 1)
                    last = pool.tensor_scalar(normed0[:, s, 0], x0[:, s, 0], negmean0[:, s, 0:1], rstd0[:, s, 0:1],
                                              ALU.add, ALU.mult)
                    last.then_inc(s_norm0_0, 1)

            run(pool, step)

        @block.scalar
        def _(act):
            def split_upper0():
                act.wait_ge(s_products, 1)
                act.activation(w_hi[:, :, KQ:KB + 1], keyq_weights, ACT.Copy).then_inc(s_upper0, 1)
                act.wait_ge(s_load_w0, 16)
                act.activation(w_hi[:, :, V0:HOP2], w_all[:, :, V0:HOP2], ACT.Copy).then_inc(s_upper0, 1)

            def split_upper1():
                act.wait_ge(s_load_w1, 16)
                act.wait_ge(s_vectors, 2)
                act.activation(w_hi[:, :, HOP2:WH], w_all[:, :, HOP2:WH], ACT.Copy).then_inc(s_upper1, 1)

            def split_upper2():
                act.wait_ge(s_load_w2, 16)
                act.wait_ge(s_vectors, 3)
                act.activation(w_hi[:, :, WH:W_COLS], w_all[:, :, WH:W_COLS], ACT.Copy).then_inc(s_upper2, 1)

            def step(t, at, live):
                if live(4):
                    p, s = pair(t, at - 4)
                    act.wait_ge(s_wh_lo, p + 1)
                    last = act.activation(wh_sb[:, s], wh[:, :, 0:D + 2], ACT.Copy)
                    last.then_inc(s_wh_out, 1)
                if live(3):
                    p, s = pair(t, at - 3)
                    act.wait_ge(s_hop1_t, p + 1)
                    last = act.activation(hop1_upper[:, s], hop1, ACT.Copy)
                    last.then_inc(s_hop1_up, 1)
                if live(1):
                    p, s = pair(t, at - 1)
                    act.wait_ge(s_val0_lo, p + 1)
                    last = act.activation(val0_sb[:, s, :, 0:1 + D], val0[:, :, 0:1 + D], ACT.Copy)
                    last.then_inc(s_val0_out, 1)
                if live(2):
                    p, s = pair(t, at - 2)
                    act.wait_ge(s_turn1_1, p + 1)
                    last = act.activation(h_hi1[:, s], turn1, ACT.Relu)
                    last.then_inc(s_hi1, 1)
                if live(1):
                    p, s = pair(t, at - 1)
                    act.wait_ge(s_kbias, p + 1)
                    act.wait_ge(s_score0, p + 1)
                    for j in range(G):
                        last = act.activation(exp0[:, s, j], score0[:, N * j:N * (j + 1)], ACT.Exp, bias=kbias[:, s, j:j + 1])
                    last.then_inc(s_exp0, 1)
                if live(5):
                    p, s = pair(t, at - 5)
                    act.wait_ge(s_turn3_0, p + 1)
                    last = act.activation(h_hi3[:, s], turn3, ACT.Relu)
                    last.then_inc(s_hi3, 1)
                if live(6):
                    p, s = pair(t, at - 6)
                    act.wait_ge(s_w3col, p + 1)
                    last = act.activation(w3col_sb[:, s], w3col, ACT.Copy)
                    last.then_inc(s_w3col_out, 1)
                if live(4):
                    p, s = pair(t, at - 4)
                    act.wait_ge(s_max2, p + 1)
                    for j in range(G):
                        last = act.activation(exp2[:, s, j], leaky2[:, s, j], ACT.Exp, bias=negmax2[:, s, j:j + 1],
                                              accum_out=sum2[:, s, j:j + 1])
                    last.then_inc(s_exp2, 1)
                if live(2):
                    p, s = pair(t, at - 2)
                    act.wait_ge(s_hop2_lo, p + 1)
                    last = act.activation(hop2_cols[:, s], hop2[:, :, D:D + 2], ACT.Copy)
                    last.then_inc(s_hop2_cols, 1)
                if live(2):
                    p, s = pair(t, at - 2)
                    if first(p):
                        split_upper2()
                    last = act.activation(hop2_upper[:, s], hop2[:, :, 0:D], ACT.Copy)
                    last.then_inc(s_hop2_up, 1)
                if live(2):
                    p, s = pair(t, at - 2)
                    act.wait_ge(s_si, p + 1)
                    act.wait_ge(s_sjrow, p + 1)
                    for j in range(G):
                        last = act.activation(z1[:, s, j], sjrow[:, N * j:N * (j + 1)], ACT.Identity, bias=si[:, s, j:j + 1])
                    last.then_inc(s_z1, 1)
                if live(5):
                    p, s = pair(t, at - 5)
                    act.wait_ge(s_vqk_lo, p + 1)
                    last = act.activation(vqk_sb[:, s], vqk[:, :, 0:D + QK], ACT.Copy)
                    last.then_inc(s_vqk_out, 1)
                if live(2):
                    p, s = pair(t, at - 2)
                    act.wait_ge(s_leaky1, p + 1)
                    last = act.activation(exp1[:, s], leaky1[:, s], ACT.Exp)
                    last.then_inc(s_exp1, 1)
                if live(4):
                    p, s = pair(t, at - 4)
                    act.wait_ge(s_mix2, p + 1)
                    last = act.activation(elu_exp[:, s], mix2, ACT.Exp)
                    last.then_inc(s_elu_exp, 1)
                if live(0):
                    p, s = pair(t, at - 0)
                    if first(p):
                        split_upper0()
                    act.wait_ge(s_turn0_0, p + 1)
                    last = act.activation(h_hi0[:, s], turn0, ACT.Relu)
                    last.then_inc(s_hi0, 1)
                if live(3):
                    p, s = pair(t, at - 3)
                    act.wait_ge(s_turn2_1, p + 1)
                    last = act.activation(h_hi2[:, s], turn2, ACT.Relu)
                    last.then_inc(s_hi2, 1)
                if live(0):
                    p, s = pair(t, at - 0)
                    act.wait_ge(s_lo0, p + 1)
                    last = act.activation(h0[:, s], turn0, ACT.Relu)
                    last.then_inc(s_h0, 1)
                if live(2):
                    p, s = pair(t, at - 2)
                    act.wait_ge(s_transT, p + 1)
                    last = act.activation(transT_upper[:, s], transT, ACT.Copy)
                    last.then_inc(s_transT_up, 1)
                if live(5):
                    p, s = pair(t, at - 5)
                    act.wait_ge(s_max3, p + 1)
                    last = act.activation(exp3[:, s], w3row, ACT.Exp, bias=negmax3[:, s], accum_out=sum3[:, s])
                    last.then_inc(s_exp3, 1)
                if live(0):
                    p, s = pair(t, at - 0)
                    if first(p):
                        split_upper1()
                    act.wait_ge(s_keyq_lo, p + 1)
                    for m in range(C):
                        last = act.activation(keyq_sb[:, s, m, :], keyq[:, m, :], ACT.Identity, bias=vectors[:, m:m + 1])
                    last.then_inc(s_keyq_out, 1)

            run(act, step)

        @block.tensor
        def _(pe):
            pe.wait_ge(s_load_setup0, 16)
            for m in range(C):
                for c in range(C):
                    pe.matmul(keyq_weights[:, m], w_setup[:, c, S_WK + P * m:S_WK + P * (m + 1)],
                              w_setup[:, c, S_WQ:S_WQ + D + 1], start=(c == 0), stop=(c == C - 1))
            for m in range(C):
                for c in range(C):
                    pe.matmul(small[:, m:m + 1], w_setup[:, c, S_WQ + P * m:S_WQ + P * (m + 1)],
                              w_setup[:, c, S_BK:S_BK + 1], start=(c == 0), stop=(c == C - 1))
            for c in range(C):
                pe.matmul(small[:, 2:3], w_setup[:, c, S_BK:S_BK + 1].broadcast_to([P, P]),
                          w_setup[:, c, S_BQ:S_BQ + 1], start=(c == 0), stop=(c == C - 1))
            pe.wait_ge(s_load_setup1, 16)
            for c in range(C):
                pe.matmul(small[:, 3:5], w_setup[:, c, S_BV1:S_BV1 + 1].broadcast_to([P, P]),
                          w_setup[:, c, S_A1:S_A1 + 2], start=(c == 0), stop=(c == C - 1))
            for m in range(C):
                for start, vectors, to in ((S_WV1, S_A1, 5), (S_WG, S_AG, 9)):
                    for c in range(C):
                        last = pe.matmul(small[:, to + 2 * m:to + 2 * m + 2],
                                         w_setup[:, c, start + P * m:start + P * (m + 1)],
                                         w_setup[:, c, vectors:vectors + 2], start=(c == 0), stop=(c == C - 1))
            last.then_inc(s_products, 1)
            pe.wait_ge(s_constants, 3)
            pe.wait_ge(s_constants_v, CONSTANTS_V)

            def transition_product(pe, out, s, j, upper, rest):
                for a, b in ((transT_upper, upper), (transT_upper, rest), (transT_rest, upper)):
                    last = pe.matmul(out, a[:, s, N * j:N * (j + 1)], b[:, s, j], start=False,
                                     stop=(j == G - 1 and a is transT_rest))
                return last

            def step(t, at, live):
                if live(6):
                    p, s = pair(t, at - 6)
                    pe.wait_ge(s_w3, p + 1)
                    last = pe.transpose(w3row, w3[:, s], ident[:, :])
                    last.then_inc(s_w3row, 1)
                if live(3):
                    p, s = pair(t, at - 3)
                    pe.wait_ge(s_trans, p + 1)
                    for j in range(G):
                        last = pe.transpose(transT[:, N * j:N * (j + 1)], trans[:, s, j], ident[:, :])
                    last.then_inc(s_transT, 1)
                if live(4):
                    p, s = pair(t, at - 4)
                    if first(p):
                        pe.wait_ge(s_lower2, 1)
                    pe.wait_ge(s_h0, upto(p + 4))
                    pe.wait_ge(s_hi2, p + 1)
                    for j in range(G):
                        last = accumulate(pe, wh[:, j, 0:D + 2], [(h_hi2[:, s, :, N * j:N * (j + 1)], w) for w in w_wh], start=True)
                if live(4):
                    p, s = pair(t, at - 4)
                    pe.wait_ge(s_lo2, p + 1)
                    for j in range(G):
                        last = accumulate(pe, wh[:, j, 0:D + 2], [(h_lo2[:, s, :, N * j:N * (j + 1)], w_wh[0])], stop=True)
                    last.then_inc(s_wh_lo, 1)
                if live(1):
                    p, s = pair(t, at - 1)
                    if first(p):
                        pe.wait_ge(s_lower0, 2)
                    if exists(p - 5):
                        pe.wait_ge(s_exp3, p - 4)
                    for j in range(G):
                        last = accumulate(pe, val0[:, j, 0:D + 2], [(h_hi0[:, s, :, N * j:N * (j + 1)], w) for w in w_v0], start=True)
                if live(3):
                    p, s = pair(t, at - 3)
                    pe.wait_ge(s_transT_rest, p + 1)
                    for j in range(G):
                        last = transition_product(pe, hop1[:, j, :], s, j, hop2_upper, hop2_rest)
                    last.then_inc(s_hop1_t, 1)
                if live(1):
                    p, s = pair(t, at - 1)
                    for j in range(G):
                        last = accumulate(pe, val0[:, j, 0:D + 2], [(h_lo0[:, s, :, N * j:N * (j + 1)], w_v0[0])], stop=True)
                    last.then_inc(s_val0_lo, 1)
                if live(2):
                    p, s = pair(t, at - 2)
                    pe.wait_ge(s_norm1_0, p + 1)
                    for c in range(C):
                        last = pe.transpose(turn1[:, c, N * 0:N * 1], normed1[:, s, 0, P * c:P * (c + 1)], ident[:, :])
                if live(2):
                    p, s = pair(t, at - 2)
                    pe.wait_ge(s_norm1_1, p + 1)
                    for c in range(C):
                        last = pe.transpose(turn1[:, c, N * 1:N * 2], normed1[:, s, 1, P * c:P * (c + 1)], ident[:, :])
                    last.then_inc(s_turn1_1, 1)
                if live(4):
                    p, s = pair(t, at - 4)
                    pe.wait_ge(s_wh_out, p + 1)
                    for j in range(G):
                        last = pe.transpose(wh1row[:, N * j:N * (j + 1)], wh_sb[:, s, j, D:D + 1].broadcast_to([N, P]), ident[:, :])
                    last.then_inc(s_wh1row, 1)
                if live(1):
                    p, s = pair(t, at - 1)
                    pe.wait_ge(s_keyq_out, p + 1)
                    for j in range(G):
                        for c in range(C):
                            last = pe.matmul(score0[:, N * j:N * (j + 1)], keyq_sb[:, s, c, N * j:N * (j + 1)],
                                             h0[:, s, c, N * j:N * (j + 1)], start=(c == 0), stop=(c == C - 1))
                    last.then_inc(s_score0, 1)
                if live(3):
                    p, s = pair(t, at - 3)
                    pe.wait_ge(s_hop1_rest, p + 1)
                    for j in range(G):
                        pe.matmul(hop0[:, j, :], ones_r[:, :], hop_bias[:, :], start=False, stop=False)
                        last = transition_product(pe, hop0[:, j, :], s, j, hop1_upper, hop1_rest)
                    last.then_inc(s_hop0_t, 1)
                if live(5):
                    p, s = pair(t, at - 5)
                    pe.wait_ge(s_norm3_1, p + 1)
                    for c in range(C):
                        last = pe.transpose(turn3[:, c, N * 1:N * 2], normed3[:, s, 1, P * c:P * (c + 1)], ident[:, :])
                if live(5):
                    p, s = pair(t, at - 5)
                    pe.wait_ge(s_norm3_0, p + 1)
                    for c in range(C):
                        last = pe.transpose(turn3[:, c, N * 0:N * 1], normed3[:, s, 0, P * c:P * (c + 1)], ident[:, :])
                    last.then_inc(s_turn3_0, 1)
                if live(6):
                    p, s = pair(t, at - 6)
                    count = held(pe, upto(p + 5))
                    pe.wait_ge(s_constants, 3)
                    pe.wait_ge(s_lo1, count)
                    pe.wait_ge(s_soft3, p + 1)
                    last = pe.transpose(w3col, soft3[:, s], ident[0:G, 0:G])
                    last.then_inc(s_w3col, 1)
                if live(2):
                    p, s = pair(t, at - 2)
                    if first(p):
                        pe.wait_ge(s_lower1, 4)
                    pe.wait_ge(s_hi1, p + 1)
                    for j in range(G):
                        last = accumulate(pe, hop2[:, j, 0:D + 2], [(h_hi1[:, s, :, N * j:N * (j + 1)], w) for w in w_hop2], start=True)
                if live(2):
                    p, s = pair(t, at - 2)
                    pe.wait_ge(s_lo1, p + 1)
                    for j in range(G):
                        last = accumulate(pe, hop2[:, j, 0:D + 2], [(h_lo1[:, s, :, N * j:N * (j + 1)], w_hop2[0])], stop=True)
                    last.then_inc(s_hop2_lo, 1)
                if live(1):
                    p, s = pair(t, at - 1)
                    pe.wait_ge(s_att0, p + 1)
                    if exists(p - 5):
                        pe.wait_ge(s_w3col_out, p - 4)
                    for j in range(G):
                        last = pe.matmul(mix0[:, j, 0:D + 1], att0[:, s, j], val0_sb[:, s, j, 1:D + 2], start=True, stop=True)
                    last.then_inc(s_mix0, 1)
                if live(5):
                    p, s = pair(t, at - 5)
                    pe.wait_ge(s_z2, upto(p + 2))
                    pe.wait_ge(s_hi3, p + 1)
                    for j in range(G):
                        last = accumulate(pe, vqk[:, j, 0:D + QK], [(h_hi3[:, s, :, N * j:N * (j + 1)], w) for w in w_vqk], start=True)
                if live(2):
                    p, s = pair(t, at - 2)
                    pe.wait_ge(s_hop2_cols, p + 1)
                    if exists(p - 3):
                        pe.wait_ge(s_lo3, p - 2)
                    for j in range(G):
                        last = pe.transpose(sjrow[:, N * j:N * (j + 1)], hop2_cols[:, s, j, 1:2].broadcast_to([N, P]), ident[:, :])
                    last.then_inc(s_sjrow, 1)
                if live(5):
                    p, s = pair(t, at - 5)
                    pe.wait_ge(s_lo3, p + 1)
                    for j in range(G):
                        last = accumulate(pe, vqk[:, j, 0:D + QK], [(h_lo3[:, s, :, N * j:N * (j + 1)], w_vqk[0])], stop=True)
                    last.then_inc(s_vqk_lo, 1)
                if live(2):
                    p, s = pair(t, at - 2)
                    if first(p):
                        pe.wait_ge(s_lower1, 4)
                    if exists(p - 1):
                        pe.wait_ge(s_x2, p)
                    for j in range(G):
                        last = accumulate(pe, hop0[:, j, :], [(h_hi1[:, s, :, N * j:N * (j + 1)], w) for w in w_hop0], start=(j == 0))
                if live(4):
                    p, s = pair(t, at - 4)
                    pe.wait_ge(s_z1, upto(p + 3))
                    pe.wait_ge(s_att2, p + 1)
                    for j in range(G):
                        last = pe.matmul(mix2[:, j, :], att2[:, s, j], wh_sb[:, s, j, 0:D], start=True, stop=True)
                    last.then_inc(s_mix2, 1)
                if live(0):
                    p, s = pair(t, at - 0)
                    pe.wait_ge(s_norm0_1, p + 1)
                    if exists(p - 5):
                        pe.wait_ge(s_vqk_out, p - 4)
                    for c in range(C):
                        last = pe.transpose(turn0[:, c, N * 1:N * 2], normed0[:, s, 1, P * c:P * (c + 1)], ident[:, :])
                if live(0):
                    p, s = pair(t, at - 0)
                    pe.wait_ge(s_norm0_0, p + 1)
                    for c in range(C):
                        last = pe.transpose(turn0[:, c, N * 0:N * 1], normed0[:, s, 0, P * c:P * (c + 1)], ident[:, :])
                    last.then_inc(s_turn0_0, 1)
                if live(2):
                    p, s = pair(t, at - 2)
                    if first(p):
                        pe.wait_ge(s_lower1, 4)
                    if exists(p - 3):
                        pe.wait_ge(s_vqk_out, p - 2)
                    for j in range(G):
                        last = accumulate(pe, hop1[:, j, :], [(h_hi1[:, s, :, N * j:N * (j + 1)], w) for w in w_hop1], start=(j == 0))
                if live(5):
                    p, s = pair(t, at - 5)
                    pe.wait_ge(s_x1, upto(p + 5))
                    pe.wait_ge(s_vqk_out, p + 1)
                    for j in range(G):
                        last = pe.matmul(adjk[:, j, :], adjT2[:, s, j], vqk_sb[:, s, j, D + ATT:D + 2 * ATT], start=True, stop=True)
                    last.then_inc(s_adjk, 1)
                if live(3):
                    p, s = pair(t, at - 3)
                    pe.wait_ge(s_hop2_rest, upto(p + 2))
                    pe.wait_ge(s_norm2_0, p + 1)
                    for c in range(C):
                        last = pe.transpose(turn2[:, c, N * 0:N * 1], normed2[:, s, 0, P * c:P * (c + 1)], ident[:, :])
                if live(3):
                    p, s = pair(t, at - 3)
                    pe.wait_ge(s_norm2_1, p + 1)
                    for c in range(C):
                        last = pe.transpose(turn2[:, c, N * 1:N * 2], normed2[:, s, 1, P * c:P * (c + 1)], ident[:, :])
                    last.then_inc(s_turn2_1, 1)
                if live(2):
                    p, s = pair(t, at - 2)
                    for j in range(G):
                        last = accumulate(pe, hop0[:, j, :], [(h_lo1[:, s, :, N * j:N * (j + 1)], w_hop0[0])], stop=False)
                if live(0):
                    p, s = pair(t, at - 0)
                    if first(p):
                        pe.wait_ge(s_lower0, 2)
                    pe.wait_ge(s_hi0, p + 1)
                    if exists(p - 1):
                        pe.wait_ge(s_x1, p)
                    for m in range(C):
                        last = accumulate(pe, keyq[:, m, :], [(w[:, :, P * m:P * (m + 1)], h_hi0[:, s]) for w in w_kq], start=(m == 0))
                if live(2):
                    p, s = pair(t, at - 2)
                    for j in range(G):
                        last = accumulate(pe, hop1[:, j, :], [(h_lo1[:, s, :, N * j:N * (j + 1)], w_hop1[0])], stop=False)
                if live(0):
                    p, s = pair(t, at - 0)
                    pe.wait_ge(s_lo0, p + 1)
                    for m in range(C):
                        last = accumulate(pe, keyq[:, m, :], [(w_kq[0][:, :, P * m:P * (m + 1)], h_lo0[:, s])], stop=(m == C - 1))
                    last.then_inc(s_keyq_lo, 1)

            run(pe, step)

        @block.vector
        def _(vec):
            vec.memset(ones_r[:, :].bitcast(F32), 1.0).then_inc(s_constants_v, 1)
            vec.memset(hop_bias[64:P, :].bitcast(F32), 0.0).then_inc(s_constants_v, 1)
            for s in range(2):
                vec.memset(val0_sb[:, s, :, D + 1], 1.0).then_inc(s_constants_v, 1)
            vec.wait_ge(s_load_bias, 16)
            for j in range(G):
                vec.tensor_scalar(value_bias[:, j, :], value_row[:, :], -1.0, None, ALU.add).then_inc(s_constants_v, 1)

            def attention_columns(start, to):
                vec.tensor_copy(w_all[:, :, to:to + 2], vectors[:, start:start + 2 * C]
                                .rearrange("p (m v) -> p m v", m=C)).then_inc(s_vectors, 1)

            def split_lower0():
                vec.wait_ge(s_products, 1)
                vec.tensor_copy(vectors[:, :], small[:, 0:13]).then_inc(s_vectors, 1)
                vec.wait_ge(s_upper0, 2)
                vec.tensor_tensor(w_lo[:, :, KQ:KB + 1], keyq_weights, w_hi[:, :, KQ:KB + 1].bitcast(F32),
                                  ALU.subtract).then_inc(s_lower0, 1)
                vec.tensor_tensor(w_lo[:, :, V0:HOP2], w_all[:, :, V0:HOP2], w_hi[:, :, V0:HOP2].bitcast(F32),
                                  ALU.subtract).then_inc(s_lower0, 1)

            def split_lower1():
                vec.wait_ge(s_vectors, 1)
                vec.wait_ge(s_load_w1, 16)
                attention_columns(5, HOP2 + D)
                vec.wait_ge(s_load_w2, 16)
                attention_columns(9, WH + D)
                vec.wait_ge(s_load_hops, 16 * 3)
                vec.tensor_scalar(sij_const[:, :], vectors[:, 3:4], vectors[:, 4:5], ab_col[:, 0:1], ALU.add,
                                  ALU.add).then_inc(s_vectors, 1)
                vec.tensor_copy(hop_bias[0:32, :], hop_rows[0:32, :]).then_inc(s_lower1, 1)
                vec.tensor_copy(hop_rows_hi[32:64, :], hop_rows[32:64, :]).then_inc(s_lower1, 1)
                vec.wait_ge(s_lower1, 2)
                vec.tensor_tensor(hop_bias[32:64, :], hop_rows[32:64, :], hop_rows_hi[32:64, :].bitcast(F32),
                                  ALU.subtract).then_inc(s_lower1, 1)
                vec.wait_ge(s_upper1, 1)
                vec.tensor_tensor(w_lo[:, :, HOP2:WH], w_all[:, :, HOP2:WH], w_hi[:, :, HOP2:WH].bitcast(F32),
                                  ALU.subtract).then_inc(s_lower1, 1)

            def split_lower2():
                vec.wait_ge(s_vectors, 4)
                vec.wait_ge(s_upper2, 1)
                vec.tensor_tensor(w_lo[:, :, WH:W_COLS], w_all[:, :, WH:W_COLS],
                                  w_hi[:, :, WH:W_COLS].bitcast(F32), ALU.subtract).then_inc(s_lower2, 1)

            def step(t, at, live):
                if live(5):
                    p, s = pair(t, at - 5)
                    vec.wait_ge(s_suminv2, p + 1)
                    last = vec.tensor_tensor(att2[:, s], exp2[:, s], suminv2[:, s].unsqueeze(2).broadcast_to([P, G, N]), ALU.mult)
                    last.then_inc(s_att2, 1)
                if live(4):
                    p, s = pair(t, at - 4)
                    vec.wait_ge(s_aggr2, p + 1)
                    vec.tensor_scalar(negmean2[:, s], moments2[:, s, :, 0], -1.0, None, ALU.mult)
                    last = vec.tensor_scalar(vareps2[:, s], moments2[:, s, :, 1], LN_EPS, None, ALU.add)
                    last.then_inc(s_mom2, 1)
                if live(2):
                    p, s = pair(t, at - 2)
                    vec.wait_ge(s_mix0, p + 1)
                    last = vec.reciprocal(rowinv0[:, s], mix0[:, :, D])
                    last.then_inc(s_rowinv0, 1)
                if live(3):
                    p, s = pair(t, at - 3)
                    vec.wait_ge(s_hop2_up, p + 1)
                    last = vec.tensor_tensor(hop2_rest[:, s], hop2[:, :, 0:D], hop2_upper[:, s].bitcast(F32), ALU.subtract)
                    last.then_inc(s_hop2_rest, 1)
                if live(7):
                    p, s = pair(t, at - 7)
                    vec.wait_ge(s_w3col_out, p + 1)
                    if exists(p - 2):
                        vec.wait_ge(s_store[s], loads(t, at - 7 - 2))
                    for j in range(G):
                        last = vec.scalar_tensor_tensor(y[:, s, j], vqk_sb[:, s, j, 0:D], w3col_sb[:, s, j:j + 1], x3[:, s, j],
                                                        ALU.mult, ALU.add)
                    last.then_inc(s_out, 1)
                if live(3):
                    p, s = pair(t, at - 3)
                    vec.wait_ge(s_z1, p + 1)
                    last = vec.scalar_tensor_tensor(leaky1[:, s], z1[:, s], SLOPE, z1[:, s], ALU.mult, ALU.max)
                    last.then_inc(s_leaky1, 1)
                if live(2):
                    p, s = pair(t, at - 2)
                    vec.wait_ge(s_rowinv0, p + 1)
                    vec.wait_ge(s_xb, p + 1)
                    for j in range(G):
                        last = vec.scalar_tensor_tensor(x1[:, s, j], mix0[:, j, 0:D], rowinv0[:, s, j:j + 1], xb[:, s, j],
                                                        ALU.mult, ALU.add)
                    last.then_inc(s_x1, 1)
                if live(3):
                    p, s = pair(t, at - 3)
                    vec.wait_ge(s_exp1, p + 1)
                    vec.wait_ge(s_load_adj1[s], loads(t, at - 3))
                    for j in range(G):
                        last = vec.scalar_tensor_tensor(alpha[:, s, j], exp1[:, s, j], 1.0, adj1[:, s, j], ALU.mult, ALU.mult,
                                                        accum_out=rowsum1[:, s, j:j + 1])
                    last.then_inc(s_alpha, 1)
                if live(2):
                    p, s = pair(t, at - 2)
                    vec.wait_ge(s_x1, p + 1)
                    for j in range(G):
                        last = vec.bn_stats(stats1[:, s, j], x1[:, s, j])
                    last.then_inc(s_stat1, 1)
                if live(3):
                    p, s = pair(t, at - 3)
                    vec.wait_ge(s_alpha, p + 1)
                    last = vec.tensor_scalar(rowsum1e[:, s], rowsum1[:, s], ROWSUM_EPS, None, ALU.add)
                    last.then_inc(s_rowsum1e, 1)
                if live(5):
                    p, s = pair(t, at - 5)
                    vec.wait_ge(s_elu_exp, p + 1)
                    last = vec.scalar_tensor_tensor(elu_pos[:, s], mix2, 0.0, x2[:, s], ALU.max, ALU.add)
                    last.then_inc(s_elu_pos, 1)
                if live(1):
                    p, s = pair(t, at - 1)
                    if first(p):
                        split_lower0()
                    vec.wait_ge(s_hi0, p + 1)
                    last = vec.scalar_tensor_tensor(h_lo0[:, s], turn0, 0.0, h_hi0[:, s].bitcast(F32), ALU.max, ALU.subtract)
                    last.then_inc(s_lo0, 1)
                if live(3):
                    p, s = pair(t, at - 3)
                    vec.wait_ge(s_rowsum1e, p + 1)
                    last = vec.reciprocal(rowinv1[:, s], rowsum1e[:, s])
                    last.then_inc(s_rowinv1, 1)
                if live(6):
                    p, s = pair(t, at - 6)
                    vec.wait_ge(s_adjk, p + 1)
                    for j in range(G):
                        last = vec.scalar_tensor_tensor(w3_prod[:, s, j], adjk[:, j, :], INV_SCALE, vqk_sb[:, s, j, D:D + ATT],
                                                        ALU.mult, ALU.mult, accum_out=w3[:, s, j:j + 1])
                    last.then_inc(s_w3, 1)
                if live(2):
                    p, s = pair(t, at - 2)
                    count = held(vec, p + 1)
                    vec.wait_ge(s_constants_v, CONSTANTS_V)
                    vec.wait_ge(s_stat1, count)
                    for j in range(G):
                        last = vec.bn_aggr(moments1[:, s, j], stats1[:, s, j])
                    last.then_inc(s_aggr1, 1)
                if live(3):
                    p, s = pair(t, at - 3)
                    vec.wait_ge(s_rowinv1, p + 1)
                    last = vec.tensor_tensor(trans[:, s], alpha[:, s], rowinv1[:, s].unsqueeze(2).broadcast_to([P, G, N]), ALU.mult)
                    last.then_inc(s_trans, 1)
                if live(5):
                    p, s = pair(t, at - 5)
                    vec.wait_ge(s_elu_pos, p + 1)
                    last = vec.scalar_tensor_tensor(x3[:, s], elu_exp[:, s], 1.0, elu_pos[:, s], ALU.min, ALU.add)
                    last.then_inc(s_x3, 1)
                if live(4):
                    p, s = pair(t, at - 4)
                    vec.wait_ge(s_hi2, p + 1)
                    last = vec.scalar_tensor_tensor(h_lo2[:, s], turn2, 0.0, h_hi2[:, s].bitcast(F32), ALU.max, ALU.subtract)
                    last.then_inc(s_lo2, 1)
                if live(2):
                    p, s = pair(t, at - 2)
                    vec.wait_ge(s_aggr1, p + 1)
                    vec.tensor_scalar(negmean1[:, s], moments1[:, s, :, 0], -1.0, None, ALU.mult)
                    last = vec.tensor_scalar(vareps1[:, s], moments1[:, s, :, 1], LN_EPS, None, ALU.add)
                    last.then_inc(s_mom1, 1)
                if live(6):
                    p, s = pair(t, at - 6)
                    vec.wait_ge(s_w3row, p + 1)
                    last = vec.tensor_reduce(negmax3[:, s], w3row, AX.X, ALU.max, negate=True)
                    last.then_inc(s_max3, 1)
                if live(0):
                    p, s = pair(t, at - 0)
                    vec.wait_ge(s_load_x[s], loads(t, at - 0))
                    for j in range(G):
                        last = vec.bn_stats(stats0[:, s, j], x0[:, s, j])
                    last.then_inc(s_stat0, 1)
                if live(3):
                    p, s = pair(t, at - 3)
                    vec.wait_ge(s_transT_up, p + 1)
                    last = vec.tensor_tensor(transT_rest[:, s], transT, transT_upper[:, s].bitcast(F32), ALU.subtract)
                    last.then_inc(s_transT_rest, 1)
                if live(5):
                    p, s = pair(t, at - 5)
                    vec.wait_ge(s_x3, p + 1)
                    for j in range(G):
                        last = vec.bn_stats(stats3[:, s, j], x3[:, s, j])
                    last.then_inc(s_stat3, 1)
                if live(0):
                    p, s = pair(t, at - 0)
                    vec.wait_ge(s_stat0, p + 1)
                if live(6):
                    p, s = pair(t, at - 6)
                    vec.wait_ge(s_exp3, p + 1)
                    last = vec.reciprocal(suminv3[:, s], sum3[:, s])
                    last.then_inc(s_suminv3, 1)
                if live(5):
                    p, s = pair(t, at - 5)
                    count = held(vec, p + 1)
                    vec.wait_ge(s_constants_v, CONSTANTS_V)
                    vec.wait_ge(s_stat3, count)
                    for j in range(G):
                        last = vec.bn_aggr(moments3[:, s, j], stats3[:, s, j])
                    last.then_inc(s_aggr3, 1)
                if live(0):
                    p, s = pair(t, at - 0)
                    for j in range(G):
                        last = vec.bn_aggr(moments0[:, s, j], stats0[:, s, j])
                    last.then_inc(s_aggr0, 1)
                if live(5):
                    p, s = pair(t, at - 5)
                    vec.wait_ge(s_aggr3, p + 1)
                    vec.tensor_scalar(negmean3[:, s], moments3[:, s, :, 0], -1.0, None, ALU.mult)
                    last = vec.tensor_scalar(vareps3[:, s], moments3[:, s, :, 1], LN_EPS, None, ALU.add)
                    last.then_inc(s_mom3, 1)
                if live(6):
                    p, s = pair(t, at - 6)
                    vec.wait_ge(s_suminv3, p + 1)
                    last = vec.tensor_scalar(soft3[:, s], exp3[:, s], suminv3[:, s], None, ALU.mult)
                    last.then_inc(s_soft3, 1)
                if live(0):
                    p, s = pair(t, at - 0)
                    vec.wait_ge(s_aggr0, p + 1)
                    vec.tensor_scalar(negmean0[:, s], moments0[:, s, :, 0], -1.0, None, ALU.mult)
                    last = vec.tensor_scalar(vareps0[:, s], moments0[:, s, :, 1], LN_EPS, None, ALU.add)
                    last.then_inc(s_mom0, 1)
                if live(4):
                    p, s = pair(t, at - 4)
                    vec.wait_ge(s_load_adjT2[s], loads(t, at - 4))
                    last = vec.tensor_scalar(penalty[:, s], adjT2[:, s], 0.5, MASKED_Z, ALU.is_le, ALU.mult)
                    last.then_inc(s_penalty, 1)
                if live(3):
                    p, s = pair(t, at - 3)
                    vec.wait_ge(s_hop1_up, p + 1)
                    last = vec.tensor_tensor(hop1_rest[:, s], hop1, hop1_upper[:, s].bitcast(F32), ALU.subtract)
                    last.then_inc(s_hop1_rest, 1)
                if live(1):
                    p, s = pair(t, at - 1)
                    if first(p):
                        split_lower1()
                    vec.wait_ge(s_val0_out, p + 1)
                    last = vec.tensor_scalar(kbias[:, s], val0_sb[:, s, :, 0], vectors[:, 2:3], None, ALU.add)
                    last.then_inc(s_kbias, 1)
                if live(4):
                    p, s = pair(t, at - 4)
                    vec.wait_ge(s_penalty, p + 1)
                    vec.wait_ge(s_wh1row, p + 1)
                    for j in range(G):
                        last = vec.scalar_tensor_tensor(z2[:, s, j], wh1row[:, N * j:N * (j + 1)], wh_sb[:, s, j, D + 1:D + 2],
                                                        penalty[:, s, j], ALU.add, ALU.add)
                    last.then_inc(s_z2, 1)
                if live(2):
                    p, s = pair(t, at - 2)
                    vec.wait_ge(s_hi1, p + 1)
                    last = vec.scalar_tensor_tensor(h_lo1[:, s], turn1, 0.0, h_hi1[:, s].bitcast(F32), ALU.max, ALU.subtract)
                    last.then_inc(s_lo1, 1)
                if live(4):
                    p, s = pair(t, at - 4)
                    vec.wait_ge(s_z2, p + 1)
                    last = vec.scalar_tensor_tensor(leaky2[:, s], z2[:, s], SLOPE, z2[:, s], ALU.mult, ALU.max)
                    last.then_inc(s_leaky2, 1)
                if live(1):
                    p, s = pair(t, at - 1)
                    vec.wait_ge(s_exp0, p + 1)
                    vec.wait_ge(s_load_adjT0[s], loads(t, at - 1))
                    last = vec.tensor_tensor(att0[:, s], exp0[:, s], adjT0[:, s], ALU.mult)
                    last.then_inc(s_att0, 1)
                if live(4):
                    p, s = pair(t, at - 4)
                    vec.wait_ge(s_leaky2, p + 1)
                    last = vec.tensor_reduce(negmax2[:, s], leaky2[:, s], AX.X, ALU.max, negate=True)
                    last.then_inc(s_max2, 1)
                if live(3):
                    p, s = pair(t, at - 3)
                    vec.wait_ge(s_hop0_t, p + 1)
                    last = vec.scalar_tensor_tensor(x2[:, s], hop0, 0.0, x1[:, s], ALU.max, ALU.add)
                    last.then_inc(s_x2, 1)
                if live(3):
                    p, s = pair(t, at - 3)
                    vec.wait_ge(s_x2, p + 1)
                    for j in range(G):
                        last = vec.bn_stats(stats2[:, s, j], x2[:, s, j])
                    last.then_inc(s_stat2, 1)
                if live(5):
                    p, s = pair(t, at - 5)
                    vec.wait_ge(s_hi3, p + 1)
                    last = vec.scalar_tensor_tensor(h_lo3[:, s], turn3, 0.0, h_hi3[:, s].bitcast(F32), ALU.max, ALU.subtract)
                    last.then_inc(s_lo3, 1)
                if live(2):
                    p, s = pair(t, at - 2)
                    if first(p):
                        split_lower2()
                    vec.wait_ge(s_hop2_cols, p + 1)
                    last = vec.tensor_scalar(si[:, s], hop2_cols[:, s, :, 0], sij_const[:, 0:1], None, ALU.add)
                    last.then_inc(s_si, 1)
                if live(4):
                    p, s = pair(t, at - 4)
                    vec.wait_ge(s_exp2, p + 1)
                    last = vec.reciprocal(suminv2[:, s], sum2[:, s])
                    last.then_inc(s_suminv2, 1)
                if live(3):
                    p, s = pair(t, at - 3)
                    count = held(vec, p + 1)
                    vec.wait_ge(s_constants_v, CONSTANTS_V)
                    vec.wait_ge(s_stat2, count)
                    for j in range(G):
                        last = vec.bn_aggr(moments2[:, s, j], stats2[:, s, j])
                    last.then_inc(s_aggr2, 1)

            run(vec, step)


def kernel(**inputs):
    import numpy as np
    import concourse.bacc as bacc
    from concourse.bass_utils import run_bass_kernel_spmd

    a = {name: np.asarray(value) for name, value in inputs.items()}
    graphs, nodes, features = a["x"].shape

    def by_pair(v):
        return np.ascontiguousarray(v.reshape(graphs // G, G, nodes, -1).transpose(0, 2, 1, 3))

    def by_half(v):
        return np.ascontiguousarray(v.reshape(features // P, P, -1).transpose(1, 0, 2))

    zeros = np.zeros((features, 2), np.float32)
    weights = np.concatenate([
        a["L0_gnn_Wv_w"].T, zeros[:, 0:1], a["L1_gnn_Wk"][2], zeros, a["L1_gnn_Wk"][1], a["L1_gnn_Wk"][0],
        a["L2_gnn_W"], zeros, a["L3_gnn_W_v"].T, a["L3_gnn_W_qk"].T], 1)
    aw, ag = a["L1_gnn_aw"].reshape(2, features), a["L2_gnn_a"].reshape(2, features)
    setup = np.concatenate([
        a["L0_gnn_Wk_w"], a["L0_gnn_Wq_w"], a["L0_gnn_Wq_b"][:, None], a["L0_gnn_Wk_b"][:, None],
        a["L1_gnn_Wv"].T, aw[::-1].T, a["L1_gnn_bv"][:, None], a["L2_gnn_W"].T, ag.T], 1)
    arrays = {
        "x_in": by_pair(a["x"]), "adj_in": by_pair(a["adj"]), "adjT_in": by_pair(a["adj"].transpose(0, 2, 1)),
        "weights_in": by_half(weights), "setup_in": by_half(setup), "hop_bias_in": a["L1_gnn_bk"],
        "value_bias_in": a["L0_gnn_Wv_b"], "ab_in": a["L1_gnn_ab"]}
    nc = bacc.Bacc("TRN2", target_bir_lowering=False, num_devices=1)
    args = [nc.dram_tensor(name, v.shape, F32, kind="ExternalInput").ap() for name, v in arrays.items()]
    y = nc.dram_tensor("y_out", arrays["x_in"].shape, F32, kind="ExternalOutput").ap()
    graph_layers_kernel(nc, *args, y)
    result = run_bass_kernel_spmd(nc, [arrays], core_ids=[0]).results[0]["y_out"]
    return np.asarray(result).transpose(0, 2, 1, 3).reshape(graphs, nodes, features)
```
